# Optimizing a Trainium2 kernel written in Bass

```python
import numpy as np
import jax
import jax.numpy as jnp

def _softmax(x, axis=-1):
    return jax.nn.softmax(x, axis=axis)

def _gelu(x):
    return jax.nn.gelu(x, approximate=True)

def _silu(x):
    return jax.nn.silu(x)

def _sigmoid(x):
    return jax.nn.sigmoid(x)

def _layernorm(x, axis=-1, eps=1e-05):
    m = jnp.mean(x, axis=axis, keepdims=True)
    v = jnp.var(x, axis=axis, keepdims=True)
    return (x - m) / jnp.sqrt(v + eps)

def _scatter_add(tgt, idx, src, axis=0):
    return tgt.at[idx].add(src)

def _segment_sum(src, seg, n):
    return jax.ops.segment_sum(src, seg, n)
kernel_name = 'mk_hybrid_d1_jaxref_r8_39ab5f'

def setup_inputs(seed: int=0):
    np.random.seed(seed)
    _w = jnp.asarray

    def _L0_attn_a_setup():
        import jax, jax.numpy as jnp
        import numpy as np
        import math
        DIM = 128
        HEADS = 16
        HEAD_DIM = DIM // HEADS
        B, N = (1, 512)
        key = jax.random.key(seed)
        k1, k2, k3, k4 = jax.random.split(key, 4)
        content = jax.random.normal(k1, (B, N, DIM), dtype=jnp.float32)
        Wq = jnp.eye(DIM, dtype=jnp.float32) + 0.02 * jax.random.normal(k2, (DIM, DIM), dtype=jnp.float32)
        Wk = jnp.eye(DIM, dtype=jnp.float32) + 0.02 * jax.random.normal(k3, (DIM, DIM), dtype=jnp.float32)
        Wv = jnp.eye(DIM, dtype=jnp.float32) + 0.02 * jax.random.normal(k4, (DIM, DIM), dtype=jnp.float32)
        return {'content': content, 'Wq': Wq, 'Wk': Wk, 'Wv': Wv}
    _L0_attn_a_in = _L0_attn_a_setup()

    def _L0_attn_b_setup():
        import jax, jax.numpy as jnp
        import numpy as np
        B, S, D = (2, 256, 128)
        H = 16
        HD = D // H
        SCALE = HD ** (-0.5)

        def _rope_tables(seq_len, dim, dtype=jnp.float32):
            inv_freq = 1.0 / 10000.0 ** (jnp.arange(0, dim, 2, dtype=jnp.float32) / dim)
            t = jnp.arange(seq_len, dtype=jnp.float32)
            freqs = t[:, None] * inv_freq[None, :]
            return (jnp.cos(freqs).astype(dtype), jnp.sin(freqs).astype(dtype))

        def _apply_rope(x, cos, sin):
            half = x.shape[-1] // 2
            x1, x2 = (x[..., :half], x[..., half:])
            c = cos[None, None, :, :]
            s = sin[None, None, :, :]
            rx1 = x1 * c - x2 * s
            rx2 = x1 * s + x2 * c
            return jnp.concatenate([rx1, rx2], axis=-1)
        key = jax.random.key(seed)
        k1, k2, k3 = jax.random.split(key, 3)
        x = jax.random.normal(k1, (B, S, D), dtype=jnp.float32)
        w_qkv = jax.random.normal(k2, (3 * D, D), dtype=jnp.float32) * D ** (-0.5)
        w_out = jax.random.normal(k3, (D, D), dtype=jnp.float32) * D ** (-0.5)
        b_out = jnp.zeros((D,), dtype=jnp.float32)
        return {'x': x, 'w_qkv': w_qkv, 'w_out': w_out, 'b_out': b_out}
    _L0_attn_b_in = _L0_attn_b_setup()

    def _L0_ffn_setup():
        import jax, jax.numpy as jnp
        import numpy as np
        NUM_EXPERTS = 8
        TOP_K = 2

        def _swiglu(x, w1, w2, w3):
            return jax.nn.silu(x @ w1) * (x @ w3) @ w2
        key = jax.random.key(seed)
        ks = jax.random.split(key, 9)
        B, S, D, H, E = (1, 128, 128, 128, NUM_EXPERTS)
        std = 0.02
        return {'x': jax.random.normal(ks[0], (B, S, D), jnp.float32), 'router_w': jax.random.normal(ks[1], (D, E), jnp.float32) * std, 'expert_bias': jnp.zeros((E,), jnp.float32), 'w1': jax.random.normal(ks[2], (E, D, H), jnp.float32) * std, 'w2': jax.random.normal(ks[3], (E, H, D), jnp.float32) * std, 'w3': jax.random.normal(ks[4], (E, D, H), jnp.float32) * std, 'sw1': jax.random.normal(ks[5], (D, H), jnp.float32) * std, 'sw2': jax.random.normal(ks[6], (H, D), jnp.float32) * std, 'sw3': jax.random.normal(ks[7], (D, H), jnp.float32) * std}
    _L0_ffn_in = _L0_ffn_setup()
    _d = {'L0_attn_a_content': _L0_attn_a_in['content'], 'L0_attn_a_Wq': _L0_attn_a_in['Wq'], 'L0_attn_a_Wk': _L0_attn_a_in['Wk'], 'L0_attn_a_Wv': _L0_attn_a_in['Wv'], 'L0_attn_b_w_qkv': _L0_attn_b_in['w_qkv'], 'L0_attn_b_w_out': _L0_attn_b_in['w_out'], 'L0_attn_b_b_out': _L0_attn_b_in['b_out'], 'L0_ffn_router_w': _L0_ffn_in['router_w'], 'L0_ffn_expert_bias': _L0_ffn_in['expert_bias'], 'L0_ffn_w1': _L0_ffn_in['w1'], 'L0_ffn_w2': _L0_ffn_in['w2'], 'L0_ffn_w3': _L0_ffn_in['w3'], 'L0_ffn_sw1': _L0_ffn_in['sw1'], 'L0_ffn_sw2': _L0_ffn_in['sw2'], 'L0_ffn_sw3': _L0_ffn_in['sw3']}
    _x0 = _d['L0_attn_a_content']
    _d['L0_attn_a_content'] = jax.random.normal(jax.random.fold_in(jax.random.key(seed), 1), (4, 1024, 128), dtype=_x0.dtype)
    del _x0
    return _d

def reference(L0_attn_a_content, L0_attn_a_Wq, L0_attn_a_Wk, L0_attn_a_Wv, L0_attn_b_w_qkv, L0_attn_b_w_out, L0_attn_b_b_out, L0_ffn_router_w, L0_ffn_expert_bias, L0_ffn_w1, L0_ffn_w2, L0_ffn_w3, L0_ffn_sw1, L0_ffn_sw2, L0_ffn_sw3):

    def _L0_attn_a_ref(content, Wq, Wk, Wv):
        import jax, jax.numpy as jnp
        import numpy as np
        import math
        DIM = 128
        HEADS = 16
        HEAD_DIM = DIM // HEADS
        B, N = (1, 512)
        b, n, d = content.shape
        Q = (content @ Wq).reshape(b, n, HEADS, HEAD_DIM)
        K = (content @ Wk).reshape(b, n, HEADS, HEAD_DIM)
        V = (content @ Wv).reshape(b, n, HEADS, HEAD_DIM)
        scores = jnp.einsum('bqhd,bkhd->bhqk', Q, K) / math.sqrt(HEAD_DIM)
        alpha = jax.nn.softmax(scores, axis=-1)
        causal = jnp.tril(jnp.ones((n, n), dtype=bool))
        alpha = jnp.where(causal, alpha, jnp.zeros((), dtype=alpha.dtype))
        Y = jnp.einsum('bhqk,bkhd->bqhd', alpha, V).reshape(b, n, d)
        return Y

    def _L0_attn_b_ref(x, w_qkv, w_out, b_out):
        import jax, jax.numpy as jnp
        import numpy as np
        B, S, D = (2, 256, 128)
        H = 16
        HD = D // H
        SCALE = HD ** (-0.5)

        def _rope_tables(seq_len, dim, dtype=jnp.float32):
            inv_freq = 1.0 / 10000.0 ** (jnp.arange(0, dim, 2, dtype=jnp.float32) / dim)
            t = jnp.arange(seq_len, dtype=jnp.float32)
            freqs = t[:, None] * inv_freq[None, :]
            return (jnp.cos(freqs).astype(dtype), jnp.sin(freqs).astype(dtype))

        def _apply_rope(x, cos, sin):
            half = x.shape[-1] // 2
            x1, x2 = (x[..., :half], x[..., half:])
            c = cos[None, None, :, :]
            s = sin[None, None, :, :]
            rx1 = x1 * c - x2 * s
            rx2 = x1 * s + x2 * c
            return jnp.concatenate([rx1, rx2], axis=-1)
        b, s, d = x.shape
        qkv = jnp.einsum('bsd,ed->bse', x, w_qkv)
        qkv = qkv.reshape(b, s, 3, H, HD).transpose(2, 0, 3, 1, 4)
        q, k, v = (qkv[0], qkv[1], qkv[2])
        cos, sin = _rope_tables(s, HD, x.dtype)
        q = _apply_rope(q, cos, sin)
        k = _apply_rope(k, cos, sin)
        scores = jnp.einsum('bhsd,bhtd->bhst', q, k) * SCALE
        attn = jax.nn.softmax(scores, axis=-1)
        out = jnp.einsum('bhst,bhtd->bhsd', attn, v)
        out = out.transpose(0, 2, 1, 3).reshape(b, s, d)
        return jnp.einsum('bsd,ed->bse', out, w_out) + b_out

    def _L0_ffn_ref(x, router_w, expert_bias, w1, w2, w3, sw1, sw2, sw3):
        import jax, jax.numpy as jnp
        import numpy as np
        NUM_EXPERTS = 8
        TOP_K = 2

        def _swiglu(x, w1, w2, w3):
            return jax.nn.silu(x @ w1) * (x @ w3) @ w2
        B, S, D = x.shape
        E, K = (NUM_EXPERTS, TOP_K)
        N = B * S
        x_flat = x.reshape(N, D)
        logits = x_flat @ router_w
        scores = jax.nn.softmax(logits.astype(jnp.float32), axis=-1)
        _, sel = jax.lax.top_k(scores + expert_bias[None, :], K)
        top_scores = jnp.take_along_axis(scores, sel, axis=-1)
        flat_exp = sel.reshape(-1)
        order = jnp.argsort(flat_exp)
        exp_sorted = flat_exp[order]
        routed_input = x_flat[order // K]
        routed_output = jnp.zeros_like(routed_input)
        for e in range(E):
            mask = (exp_sorted == e)[:, None]
            y_e = _swiglu(routed_input, w1[e], w2[e], w3[e])
            routed_output = routed_output + jnp.where(mask, y_e, 0.0)
        unsorted = jnp.zeros((N * K, D), routed_output.dtype).at[order].set(routed_output)
        unsorted = unsorted.reshape(N, K, D)
        out_experts = jnp.einsum('nk,nkd->nd', top_scores, unsorted)
        shared_out = _swiglu(x_flat, sw1, sw2, sw3)
        return (shared_out + out_experts).reshape(B, S, D)
    x = L0_attn_a_content
    x = x + _L0_attn_a_ref(_layernorm(x, axis=-1), L0_attn_a_Wq, L0_attn_a_Wk, L0_attn_a_Wv)
    x = x + _L0_ffn_ref(_layernorm(x, axis=-1), L0_ffn_router_w, L0_ffn_expert_bias, L0_ffn_w1, L0_ffn_w2, L0_ffn_w3, L0_ffn_sw1, L0_ffn_sw2, L0_ffn_sw3)
    x = x + _L0_attn_b_ref(_layernorm(x, axis=-1), L0_attn_b_w_qkv, L0_attn_b_w_out, L0_attn_b_b_out)
    x = x + _L0_ffn_ref(_layernorm(x, axis=-1), L0_ffn_router_w, L0_ffn_expert_bias, L0_ffn_w1, L0_ffn_w2, L0_ffn_w3, L0_ffn_sw1, L0_ffn_sw2, L0_ffn_sw3)
    return x

_drawn_inputs = setup_inputs


def setup_inputs(seed=0):
    import zlib

    import numpy as np

    out = dict(_drawn_inputs(seed))
    spreads = {'L0_attn_b_b_out': (0.0, 0.1), 'L0_ffn_expert_bias': (0.0, 0.8)}
    factors = {'L0_ffn_router_w': 8.0,
     'L0_ffn_w1': 8.0,
     'L0_ffn_w2': 8.0,
     'L0_ffn_w3': 8.0,
     'L0_ffn_sw1': 6.003,
     'L0_ffn_sw2': 5.967,
     'L0_ffn_sw3': 5.881}
    for name, (base, spread) in spreads.items():
        noise = np.random.default_rng([zlib.crc32(name.encode()), seed]).standard_normal(out[name].shape)
        drawn = base * np.exp(spread * noise) if base else spread * noise
        out[name] = jnp.asarray(drawn.astype(out[name].dtype))
    for name, factor in factors.items():
        out[name] = (out[name] * factor).astype(out[name].dtype)
    return out
```

```python
from contextlib import ExitStack

import numpy as np

import concourse.bass as bass
from concourse import mybir

F32 = mybir.dt.float32
BF16 = mybir.dt.bfloat16
ALU = mybir.AluOpType
ACT = mybir.ActivationFunctionType
AX = mybir.AxisListType

P = 128
B = 4
S = 1024
D = 128
HD = 8
NG = 4
GH = 4
GR = GH * HD
NT = S // P
TILES = B * NT
CHUNK = 512
CT = CHUNK // P
HALVES = S // CHUNK
E = 8
NE = E + 1
PARTS = 3
PR = 32
MAXROW = PARTS * PR
VW = (HD + 1) * GH
EPS = 1e-5
SCALE = float(HD) ** -0.5
DMA = 16


class Buffers:
    pass


def allocate(nc, ctx):
    m = Buffers()

    def sb(name, shape, dt=F32):
        return ctx.enter_context(nc.sbuf_tensor(name, shape, dt))

    m.x = sb("x", [P, TILES * D])
    m.attn = sb("attn", [P, TILES * D])
    m.ident = sb("ident", [P, P])
    m.w_q = sb("w_q", [P, 2, 2, D])
    m.w_v = sb("w_v", [P, D])
    m.w_out = sb("w_out", [P, D])
    m.b_out = sb("b_out", [P, D])
    m.rope = m.attn[:, 0:2 * S].rearrange("p (k s) -> p k s", k=2)
    m.w_router = sb("w_router", [P, E])
    m.e_bias = sb("e_bias", [P, E])
    m.w1 = sb("w1", [P, NE, D])
    m.w2 = sb("w2", [P, NE, D])
    m.w3 = sb("w3", [P, NE, D])
    m.gates = sb("gates", [P, TILES, NE])
    m.xn = sb("xn", [P, 2, CHUNK])
    m.xt = sb("xt", [P, 2, CHUNK])
    m.stats = sb("stats", [P, 2, CT, 6])
    m.mv = sb("mv", [P, 2, CT, 2])
    m.rstd = sb("rstd", [P, 2, CT])
    m.expo = sb("expo", [P, CT])
    m.qx = sb("qx", [P, NG, GH, S], BF16)
    m.kx = sb("kx", [P, NG, GH, S], BF16)
    m.probs = sb("probs", [P, 4, GH, S])
    m.room = m.probs[:, :, :, :].rearrange("p a h s -> p (a h s)")
    m.vg = sb("vg", [P, NG, NT, VW])
    m.causal = sb("causal", [P, P])
    m.w01 = sb("w01", [P, HD + 1])
    m.psS = ctx.enter_context(nc.psum_tensor("psS", [P, 2, CHUNK], F32))
    m.psT = ctx.enter_context(nc.psum_tensor("psT", [P, 2, 2 * CHUNK], F32))
    m.psO = ctx.enter_context(nc.psum_tensor("psO", [P, 2, CHUNK], F32))
    m.q_parts = nc.dram_tensor("q_parts", (B, PARTS, P, S), BF16, kind="Internal").ap()
    m.k_parts = nc.dram_tensor("k_parts", (B, PARTS, P, S), BF16, kind="Internal").ap()
    m.v_rows = nc.dram_tensor("v_rows", (B, NG, NT, P, GR), F32, kind="Internal").ap()
    return m


def tile_cols(tile):
    return bass.ds(tile * D, D)


def chunk_cols(chunk):
    return bass.ds(chunk * CHUNK, CHUNK)


def hold(eng, sem, value, passed):
    eng.wait_ge(sem, value)
    eng.sem_inc(passed, 1)


def setup(nc, m, a):
    with ExitStack() as ctx:
        loaded = ctx.enter_context(nc.semaphore("loaded"))
        cleared = ctx.enter_context(nc.semaphore("cleared"))
        zeroed = ctx.enter_context(nc.semaphore("zeroed"))
        block = ctx.enter_context(nc.Block())
        loads = [
            (m.x[:, :].rearrange("p (t d) -> p t d", d=D), a["x"].rearrange("b (t p) d -> p (b t) d", p=P)),
            (m.w_q[:, 0, 0, :], a["a_wq"]),
            (m.w_q[:, 1, 0, :], a["a_wk"]),
            (m.w_v[:, :], a["a_wv"]),
            (m.w_out[:, :], a["b_wout"]),
            (m.b_out[:, :], a["b_bias"].partition_broadcast(P)),
            (m.w_router[:, :], a["router"]),
            (m.e_bias[:, :], a["e_bias"].partition_broadcast(P)),
        ]
        for w, routed, shared in ((m.w1, "w1", "sw1"), (m.w3, "w3", "sw3"), (m.w2, "w2", "sw2")):
            loads.append((w[:, 0:E, :], a[routed].rearrange("e i o -> i e o")))
            loads.append((w[:, E, :], a[shared]))

        @block.sync
        def _(sp):
            for out, src in loads:
                sp.dma_start(out, src).then_inc(loaded, DMA)
            sp.wait_ge(loaded, DMA * len(loads))

        @block.gpsimd
        def _(pool):
            pool.memset(m.ident[:, :], 0.0).then_inc(cleared, 1)
            pool.memset(m.w01[:, :], 0.0).then_inc(cleared, 1)
            pool.memset(m.causal[:, :], 1.0).then_inc(cleared, 1)
            pool.memset(m.expo[:, :], -0.5)
            pool.memset(m.vg[:, :, :, GR:VW], 1.0)
            pool.memset(m.gates[:, :, E:NE], 1.0)
            pool.wait_ge(cleared, 3)
            pool.affine_select(out=m.causal[:, :], in_=m.causal[:, :], compare_op=ALU.is_ge, fill=0.0,
                               base=0, pattern=[[1, P]], channel_multiplier=-1)
            pool.affine_select(out=m.ident[:, :], in_=m.ident[:, :], compare_op=ALU.not_equal, fill=1.0,
                               base=0, pattern=[[-1, P]], channel_multiplier=1)
            pool.memset(m.w01[:, HD:HD + 1], 1.0)

        @block.vector
        def _(dve):
            dve.memset(m.qx[:, :, :, :], 0.0).then_inc(zeroed, 1)
            dve.memset(m.kx[:, :, :, :], 0.0).then_inc(zeroed, 1)
            dve.memset(m.psO[:, :, :], 0.0)
            dve.wait_ge(zeroed, 2)
            dve.memset(m.kx[MAXROW:MAXROW + PARTS, :, :, :], 1.0)


def norm_semaphores(nc, ctx, tag):
    def sem(name):
        return ctx.enter_context(nc.semaphore(f"{tag}_{name}"))

    s = Buffers()
    s.moments = sem("moments")
    s.stats_done = sem("stats_done")
    s.shifted = sem("shifted")
    s.rstd_done = sem("rstd_done")
    s.xn_done = sem("xn_done")
    s.turned = sem("turned")
    s.xt_done = sem("xt_done")
    s.passed_dve = sem("passed_dve")
    s.passed_pool = sem("passed_pool")
    return s


def norm_dve_moments(nc, dve, m, s, chunk, h):
    for t in range(CT):
        dve.bn_stats(m.stats[:, h, t, :], m.x[:, tile_cols(chunk * CT + t)]).then_inc(s.moments, 1)
    hold(dve, s.moments, chunk * CT + CT, s.passed_dve)
    for t in range(CT):
        dve.bn_aggr(m.mv[:, h, t, :], m.stats[:, h, t, :]).then_inc(s.stats_done, 1)


def norm_pool_rstd(nc, pool, m, s, chunk, h):
    hold(pool, s.stats_done, chunk * CT + CT, s.passed_pool)
    pool.tensor_scalar(m.rstd[:, h, :], m.mv[:, h, :, 1], EPS, 0.0, ALU.add, ALU.add).then_inc(s.shifted, 1)
    pool.wait_ge(s.shifted, chunk + 1)
    pool.tensor_tensor(m.rstd[:, h, :], m.rstd[:, h, :], m.expo[:, :], ALU.pow).then_inc(s.rstd_done, 1)


def norm_dve_apply(nc, dve, m, s, chunk, h):
    dve.wait_ge(s.stats_done, chunk * CT + CT)
    dve.wait_ge(s.rstd_done, chunk + 1)
    for t in range(CT):
        dve.tensor_scalar(m.xn[:, h, t * P:(t + 1) * P], m.x[:, tile_cols(chunk * CT + t)],
                          m.mv[:, h, t, 0:1], m.rstd[:, h, t:t + 1],
                          ALU.subtract, ALU.mult).then_inc(s.xn_done, 1)


def norm_pe_turn(nc, pe, m, s, chunk, h):
    pe.wait_ge(s.xn_done, chunk * CT + CT)
    for t in range(CT):
        last = pe.transpose(m.psS[:, h, t * P:(t + 1) * P], m.xn[:, h, t * P:(t + 1) * P], m.ident[:, :])
    last.then_inc(s.turned, 1)


def over_chunks(eng, body):
    with eng.Fori(0, B - 1) as b:
        for h in range(2):
            body(b * 2 + h, h, True)
    for h in range(2):
        body(2 * (B - 1) + h, h, h == 0)


def project(nc, m, layer, weights):
    rope = layer == "b"
    with ExitStack() as ctx:
        def sem(name):
            return ctx.enter_context(nc.semaphore(f"{layer}p_{name}"))

        s = norm_semaphores(nc, ctx, f"{layer}p")
        w_loaded = sem("w_loaded")
        qk_done = sem("qk_done")
        v_done = sem("v_done")
        v_copied = sem("v_copied")
        turned_q = sem("turned_q")
        rotated = sem("rotated")
        high = sem("high")
        rest1 = sem("rest1")
        middle = sem("middle")
        low = sem("low")
        stored = [sem(f"stored{h}") for h in range(2)]
        staging_free = sem("staging_free")
        room = m.room
        rest = room[:, 0:1024]
        prod_c, prod_s = room[:, 1024:2048], room[:, 2048:3072]
        full = room[:, 3072:4096]
        vbuf = room[:, 4096:5120].rearrange("p (h n) -> p h n", h=2)
        pbuf = room[:, 5120:8192].bitcast(BF16).rearrange("p (h c n) -> p h c n", h=2, c=PARTS)
        qk = m.psT[:, 0, :]
        qk_swapped = m.psT[:, 1, :]
        block = ctx.enter_context(nc.Block())

        @block.sync
        def _(sp):
            for out, src in weights:
                sp.dma_start(out, src).then_inc(w_loaded, DMA)
            sp.sem_inc(staging_free, 2)

            def body(b, h):
                chunk = b * 2 + h
                sp.wait_ge(low, chunk + 1)
                sp.wait_ge(middle, chunk + 1)
                for c in range(PARTS):
                    for i, dst in enumerate((m.q_parts, m.k_parts)):
                        out = dst[bass.ds(b, 1), c, :, h * CHUNK:(h + 1) * CHUNK].rearrange("b p n -> (b p) n")
                        sp.dma_start(out, pbuf[:, h, c, i * CHUNK:(i + 1) * CHUNK]).then_inc(stored[h], DMA)
                sp.wait_ge(v_copied, chunk + 1)
                for t in range(CT):
                    out = m.v_rows[bass.ds(b, 1), :, h * CT + t, :, :].rearrange("b g p r -> p (b g) r")
                    sp.dma_start(out, vbuf[:, h, t * D:(t + 1) * D].rearrange("p (g r) -> p g r", g=NG)
                                 ).then_inc(stored[h], DMA)
                sp.wait_ge(stored[h], (b + 1) * (DMA * (2 * PARTS + CT)))
                sp.sem_inc(staging_free, 1)

            with sp.Fori(0, B) as b:
                for h in range(2):
                    body(b, h)

        @block.gpsimd
        def _(pool):
            norm_pool_rstd(nc, pool, m, s, 0, 0)

            def body(chunk, h, more):
                if more:
                    norm_pool_rstd(nc, pool, m, s, chunk + 1, 1 - h)
                if rope:
                    pool.wait_ge(turned_q, chunk * 2 + 2)
                    pool.tensor_tensor(full, prod_c, prod_s, ALU.add).then_inc(rotated, 1)

            over_chunks(pool, body)

        @block.vector
        def _(dve):
            norm_dve_moments(nc, dve, m, s, 0, 0)
            norm_dve_apply(nc, dve, m, s, 0, 0)

            def body(chunk, h, more):
                if more:
                    norm_dve_moments(nc, dve, m, s, chunk + 1, 1 - h)
                dve.wait_ge(qk_done, chunk + 1)
                source = qk
                if rope:
                    for n, (ps, out) in enumerate(((qk, prod_c), (qk_swapped, prod_s))):
                        table = m.rope[:, n, h * CHUNK:(h + 1) * CHUNK].unsqueeze(1).to_broadcast([P, 2, CHUNK])
                        dve.tensor_tensor(out.rearrange("p (i n) -> p i n", i=2),
                                          ps.rearrange("p (i n) -> p i n", i=2), table,
                                          ALU.mult).then_inc(turned_q, 1)
                    source = full
                if more:
                    norm_dve_apply(nc, dve, m, s, chunk + 1, 1 - h)
                dve.wait_ge(high, chunk + 1)
                dve.tensor_tensor(rest, source, pbuf[:, h, 0, :], ALU.subtract).then_inc(rest1, 1)
                dve.wait_ge(middle, chunk + 1)
                dve.wait_ge(rest1, chunk + 1)
                dve.tensor_tensor(pbuf[:, h, 2, :], rest, pbuf[:, h, 1, :], ALU.subtract).then_inc(low, 1)
                dve.wait_ge(low, chunk + 1)

            over_chunks(dve, body)

        @block.scalar
        def _(act):
            def body(chunk, h, more):
                act.wait_ge(s.turned, chunk + 1)
                act.activation(m.xt[:, h, :], m.psS[:, h, :], ACT.Copy).then_inc(s.xt_done, 1)
                act.wait_ge(staging_free, chunk + 1)
                if rope:
                    act.wait_ge(rotated, chunk + 1)
                else:
                    act.wait_ge(qk_done, chunk + 1)
                act.activation(pbuf[:, h, 0, :], full if rope else qk, ACT.Copy).then_inc(high, 1)
                act.wait_ge(v_done, chunk + 1)
                act.activation(vbuf[:, h, :], m.psO[:, h, :], ACT.Copy).then_inc(v_copied, 1)
                act.wait_ge(rest1, chunk + 1)
                act.activation(pbuf[:, h, 1, :], rest, ACT.Copy).then_inc(middle, 1)

            over_chunks(act, body)

        @block.tensor
        def _(pe):
            pe.wait_ge(w_loaded, DMA * len(weights)) if weights else None

            def body(chunk, h, more, first=False):
                norm_pe_turn(nc, pe, m, s, chunk, h)
                pe.wait_ge(s.xt_done, chunk + 1)
                for t in range(CT):
                    last = pe.matmul(m.psO[:, h, t * D:(t + 1) * D], m.xt[:, h, t * P:(t + 1) * P],
                                     m.w_v[:, :], start=True, stop=True, skip_group_check=True)
                last.then_inc(v_done, 1)
                if not first:
                    pe.wait_ge(turned_q if rope else rest1, chunk * 2 if rope else chunk)
                for swapped in range(2 if rope else 1):
                    for i in range(2):
                        last = pe.matmul(m.psT[:, swapped, i * CHUNK:(i + 1) * CHUNK],
                                         m.w_q[:, i, swapped, :], m.xt[:, h, :], start=True, stop=True)
                last.then_inc(qk_done, 1)

            body(0, 0, True, first=True)
            with pe.Fori(0, B - 1) as b:
                body(b * 2 + 1, 1, True)
                body(b * 2 + 2, 0, True)
            body(2 * B - 1, 1, False)


def attend(nc, m, layer):
    masked_after = layer == "a"
    n_groups = B * NG
    order = list(range(NT - 1, -1, -1))
    LOADS = 2 * PARTS * PARTS + 1
    ITEMS = NG * 16 + 3
    with ExitStack() as ctx:
        def sem(name):
            return ctx.enter_context(nc.semaphore(f"{layer}t_{name}"))

        def sb(name, shape, dt=F32):
            return ctx.enter_context(nc.sbuf_tensor(f"{layer}t_{name}", shape, dt))

        group_loaded = [sem(f"group_loaded{g}") for g in range(NG)]
        s_filled = sem("s_filled")
        s_read = sem("s_read")
        max_ready = sem("max_ready")
        split = sem("split")
        max_loaded = sem("max_loaded")
        t_filled = sem("t_filled")
        exp_done = sem("exp_done")
        masked = sem("masked")
        pv_done = sem("pv_done")
        o_copied = sem("o_copied")
        o_step = sem("o_step")
        passed = sem("passed")
        passed_dve = sem("passed_dve")
        rmax = sb("rmax", [P, 2, GH * NT, 2])
        negmax = sb("negmax", [P, 2, GH * NT])
        turned_max = sb("turned_max", [GH * NT, P])
        left = sb("left", [GH * NT, P])
        mparts = sb("mparts", [GH * NT, PARTS, P], BF16)
        sums = sb("sums", [P, 2, CHUNK])
        recip = sb("recip", [P, CT * GH])
        heads = sb("heads", [P, CT, GH, HD])
        pdiag = sb("pdiag", [P, 2, GH, P])
        block = ctx.enter_context(nc.Block())

        def stream(n):
            return [(n + 1 + (8 + i) // 32, (8 + i) // 8 % GH, i % 8) for i in range(32)]

        def s_order(n, first, scores):
            out = []
            for step in range(32):
                if step < scores:
                    out.append((step, "score", step))
                if step == 8 and not first:
                    out.append((step, "turn", 0))
                if step == 10 and not first:
                    out.append((step, "turn", 1))
                if step == 25 and scores >= 24:
                    out.append((step, "max", 0))
            return out

        PRO = 32 * 2 + 1 + 16

        def scores_beside(n_left):
            return 32 if n_left >= 3 else 24 if n_left == 2 else 0

        def s_before(n, n_left, first):
            if first:
                return PRO
            return n * ITEMS + PRO - 2 - (16 if n_left == 1 else 0)

        def expand(items):
            return [(h, item) for item in items for h in range(2 if item[1] == "score" else 1)]

        def parity_of(g, first):
            return s_before(g if g else NG, NG, first) % 2

        def s_end():
            return s_before(n_groups - 1, 1, False) + 2

        def parity_end():
            return s_end() % 2

        @block.sync
        def _(sp):
            def load(b, g):
                for p in range(PARTS):
                    for c in range(PARTS):
                        r = p * PR + c * HD
                        for dst, src, part in ((m.qx, m.q_parts, p), (m.kx, m.k_parts, c)):
                            rows = src[bass.ds(b, 1), part, g * GR:(g + 1) * GR, :]
                            sp.dma_start(dst[r:r + HD, g, :, :].rearrange("p h s -> p (h s)"),
                                         rows.rearrange("b (d h) s -> (b d) (h s)", h=GH)
                                         ).then_inc(group_loaded[g], DMA)
                sp.dma_start(m.vg[:, g, :, 0:GR],
                             m.v_rows[bass.ds(b, 1), g, :, :, :].rearrange("b t p r -> p (b t) r")
                             ).then_inc(group_loaded[g], DMA)

            def maxima(n, g):
                sp.wait_ge(split, 4 * n + 4)
                for c in range(PARTS):
                    sp.dma_start(m.qx[MAXROW + c:MAXROW + c + 1, g, :, :].rearrange("p h (t q) -> p (h t) q", q=P),
                                 mparts[:, c, :]).then_inc(max_loaded, DMA)

            def body(b, g, n_left):
                n = b * NG + g
                if n_left >= 4:
                    sp.wait_ge(pv_done, 16 * n)
                    load(b + (g + 3) // NG, (g + 3) % NG)
                if n_left >= 2:
                    maxima(n + 1, (g + 1) % NG)

            for g in range(3):
                load(0, g)
            maxima(0, 0)
            load(0, 3)
            maxima(1, 1)
            with sp.Fori(0, B - 1) as b:
                for g in (1, 2, 3):
                    body(b, g, 5)
                body(b + 1, 0, 5)
            for g in (1, 2, 3):
                body(B - 1, g, NG - g)

        @block.gpsimd
        def _(pool):
            def split_max(n, uses, first=False):
                hold(pool, s_read, uses, passed)
                if not first:
                    hold(pool, max_loaded, DMA * PARTS * n, passed)
                pool.tensor_copy(mparts[:, 0, :], turned_max[:, :]).then_inc(split, 1)
                pool.wait_ge(split, 4 * n + 1)
                pool.tensor_tensor(left[:, :], turned_max[:, :], mparts[:, 0, :], ALU.subtract).then_inc(split, 1)
                hold(pool, split, 4 * n + 2, passed)
                pool.tensor_copy(mparts[:, 1, :], left[:, :]).then_inc(split, 1)
                pool.wait_ge(split, 4 * n + 3)
                pool.tensor_tensor(mparts[:, 2, :], left[:, :], mparts[:, 1, :], ALU.subtract).then_inc(split, 1)

            def body(b, g, n_left, first=False):
                n = b * NG + g
                for jj, j in enumerate(order):
                    if masked_after:
                        pool.wait_ge(exp_done, n * 32 + jj * 4 + 4)
                        if not (first and jj < 2):
                            pool.wait_ge(pv_done, n * 16 + 2 * jj - 2)
                        pool.tensor_tensor(pdiag[:, jj % 2, :, :], m.probs[:, jj % 4, :, j * P:(j + 1) * P],
                                           m.causal[:, :].unsqueeze(1).to_broadcast([P, GH, P]),
                                           ALU.mult).then_inc(masked, 1)
                    if jj == 5 and n_left >= 2:
                        uses = 2 * min(26, scores_beside(n_left)) + (0 if first else 2) + 1
                        split_max(n + 1, s_before(n, n_left, first) + uses)

            split_max(0, 2 * GH * NT + 1, first=True)
            body(0, 0, 9, first=True)
            with pool.Fori(0, B - 1) as b:
                for g in (1, 2, 3):
                    body(b, g, 9)
                body(b + 1, 0, 9)
            for g in (1, 2, 3):
                body(B - 1, g, NG - g)

        @block.scalar
        def _(act):
            def body(b, g, n_left, first=False):
                n = b * NG + g
                for jj in range(NT):
                    if not (first and jj < 4):
                        act.wait_ge(pv_done, n * 16 + 2 * (jj - 3))
                    for hh in range(GH):
                        act.wait_ge(t_filled, n * 32 + jj * 4 + hh + 1)
                        act.activation(m.probs[:, jj % 4, hh, :], m.psT[:, hh % 2, :], ACT.Exp,
                                       scale=SCALE).then_inc(exp_done, 1)
                        if jj == 1 and hh < 2 and not first:
                            copy_sums(n, hh)

            def copy_sums(n, half):
                act.wait_ge(pv_done, n * 16 - 1 + half)
                act.activation(sums[:, half, :], m.psO[:, half, :], ACT.Copy).then_inc(o_copied, 1)

            body(0, 0, 9, first=True)
            with act.Fori(0, B - 1) as b:
                for g in (1, 2, 3):
                    body(b, g, 9)
                body(b + 1, 0, 9)
            for g in (1, 2, 3):
                body(B - 1, g, NG - g)
            for half in range(2):
                copy_sums(n_groups, half)

        @block.vector
        def _(dve):
            def combine(parity, count):
                dve.wait_ge(s_read, count)
                dve.tensor_reduce(negmax[:, parity, :], rmax[:, parity, :, :], AX.X, ALU.max,
                                  negate=True).then_inc(max_ready, 1)

            def copy_max(bank, count, n, first=False):
                dve.wait_ge(s_filled, count + 1)
                if not first:
                    dve.wait_ge(split, 4 * n)
                dve.tensor_copy(turned_max[:, :], m.psS[0:GH * NT, bank, 0:P]).then_inc(s_read, 1)

            def finish(n, pb, pg, half, bank, count):
                dve.wait_ge(s_filled, count + 1)
                src = m.psS[:, bank, :].rearrange("p (t h r) -> p t h r", t=CT, h=GH)
                before = n * 6 + half * 3
                dve.reciprocal(recip[:, :].rearrange("p (t h o) -> p t h o", t=CT, h=GH),
                               src[:, :, :, HD:HD + 1]).then_inc(o_step, 1)
                dve.wait_ge(o_step, before + 1)
                scale = recip[:, :].rearrange("p (t h o) -> p t h o", t=CT, h=GH).to_broadcast([P, CT, GH, HD])
                dve.tensor_tensor(heads[:, :, :, :], src[:, :, :, 0:HD], scale, ALU.mult).then_inc(s_read, 1)
                hold(dve, s_read, count + 1, passed_dve)
                dest = m.x if masked_after else m.attn
                cols = dest[:, bass.ds(pb * (NT * D) + half * (CT * D), CT * D)]
                cols = cols.rearrange("p (t d) -> p t d", t=CT)[:, :, pg * GR:(pg + 1) * GR]
                flat = heads[:, :, :, :].rearrange("p t h d -> p t (h d)")
                if masked_after:
                    dve.tensor_tensor(cols, cols, flat, ALU.add).then_inc(o_step, 2)
                else:
                    dve.tensor_copy(cols, flat).then_inc(o_step, 2)

            def body(b, g, n_left, first=False):
                n = b * NG + g
                base = s_before(n, n_left, first)
                par0 = (g + 1) % 2
                scores = scores_beside(n_left)
                pb, pg = (b, g - 1) if g else (b - 1, NG - 1)
                off = parity_of(g, first)
                steps = stream(0)
                for k, (item, (_, kind, v)) in enumerate(expand(s_order(n, first, scores))):
                    count, bank = base + k, (off + k) % 2
                    if kind == "score":
                        ahead, hh, i = steps[v]
                        par = (par0 + ahead - 1) % 2
                        dve.wait_ge(s_filled, count + 1)
                        dve.tensor_reduce(rmax[:, par, hh * NT + i, item:item + 1], m.psS[:, bank, :],
                                          AX.X, ALU.max).then_inc(s_read, 1)
                        if v == 23 and item == 1:
                            combine(par0, count + 1)
                    elif kind == "turn":
                        finish(n - 1, pb, pg, v, bank, count)
                    else:
                        copy_max(bank, count, n + 1)

            count = 0
            for grp, hh, i in [(0, hh, i) for hh in range(GH) for i in range(NT)] + [(1, 0, i) for i in range(NT)]:
                for half in range(2):
                    dve.wait_ge(s_filled, count + 1)
                    dve.tensor_reduce(rmax[:, grp, hh * NT + i, half:half + 1], m.psS[:, count % 2, :],
                                      AX.X, ALU.max).then_inc(s_read, 1)
                    count += 1
                if count == 64:
                    combine(0, 64)
                    copy_max(0, 64, 0, first=True)
                    count += 1
            body(0, 0, 9, first=True)
            with dve.Fori(0, B - 1) as b:
                for g in (1, 2, 3):
                    body(b, g, 9)
                body(b + 1, 0, 9)
            for g in (1, 2, 3):
                body(B - 1, g, NG - g)
            end = s_end()
            for half in range(2):
                finish(n_groups - 1, B - 1, NG - 1, half, (parity_end() + half) % 2, end + half)

        @block.tensor
        def _(pe):
            def score(g, hh, i, half, bank):
                return pe.matmul(m.psS[:, bank, :], m.qx[0:MAXROW, g, hh, i * P:(i + 1) * P],
                                 m.kx[0:MAXROW, g, hh, half * CHUNK:(half + 1) * CHUNK], start=True, stop=True)

            def bank_free(count):
                if not isinstance(count, int) or count >= 2:
                    pe.wait_ge(s_read, count - 1)

            def turn_max(parity, bank, count, n):
                pe.wait_ge(max_ready, n + 1)
                bank_free(count)
                pe.transpose(m.psS[0:GH * NT, bank, 0:P], negmax[:, parity, :], m.ident[:, :]).then_inc(s_filled, 1)

            def turn_sums(n, half, bank, count):
                pe.wait_ge(o_copied, 2 * n + 1 + half)
                bank_free(count)
                for t in range(CT):
                    last = pe.transpose(m.psS[:, bank, t * P:(t + 1) * P], sums[:, half, t * P:(t + 1) * P],
                                        m.ident[:, :])
                last.then_inc(s_filled, 1)

            def weigh(n, g, jj, half, first):
                j = order[jj]
                if jj == 0 and not first:
                    pe.wait_ge(o_copied, 2 * n - 1 + half)
                lo, hi, edge = half * CHUNK, (half + 1) * CHUNK, (j + 1) * P
                pe.wait_ge(exp_done, n * 32 + jj * 4 + 4)
                if not masked_after:
                    pieces = [("all", lo, hi)]
                else:
                    pieces = []
                    if min(hi, edge) > lo:
                        pieces.append(("ones", lo, min(hi, edge)))
                    if hi > max(lo, edge):
                        pieces.append(("all", max(lo, edge), hi))
                    if lo <= j * P < hi:
                        pe.wait_ge(masked, n * 8 + jj + 1)
                        pieces.append(("diagonal", j * P, edge))
                for k, (kind, q0, q1) in enumerate(pieces):
                    rows = HD if kind == "diagonal" else HD + 1
                    for hh in range(GH):
                        w = m.w01[:, :] if kind == "ones" else m.vg[:, g, j, hh:hh + GH * (rows - 1) + 1:GH]
                        src = pdiag[:, jj % 2, hh, :] if kind == "diagonal" else m.probs[:, jj % 4, hh, q0:q1]
                        last = pe.matmul(m.psO[32 * hh:32 * hh + rows, half, q0 - lo:q1 - lo], w, src,
                                         start=jj == 0 and k == 0, stop=jj == NT - 1 and k == len(pieces) - 1,
                                         skip_group_check=True)
                last.then_inc(pv_done, 1)

            plan = {(2, 1): [(0, 0)], (2, 3): [(0, 1)],
                    (3, 0): [(1, 0)], (3, 1): [(1, 1)], (3, 2): [(2, 0)], (3, 3): [(2, 1)]}
            for jj in range(4, NT):
                plan[(jj, 1)] = [(jj - 1, 0)]
                plan[(jj, 3)] = [(jj - 1, 1)]

            def body(b, g, n_left, first=False):
                n = b * NG + g
                scores = scores_beside(n_left)
                base = s_before(n, n_left, first)
                off = parity_of(g, first)
                uses = expand(s_order(n, first, scores))
                steps = stream(0)
                k = 0
                for jj, j in enumerate(order):
                    for hh in range(GH):
                        step = jj * GH + hh
                        while k < len(uses) and uses[k][1][0] == step:
                            half, (_, kind, v) = uses[k]
                            count, bank = base + k, (off + k) % 2
                            if kind == "score":
                                ahead, sh, i = steps[v]
                                sg = (g + ahead) % NG
                                if v % 8 == 0 and half == 0 and sh == 0:
                                    pe.wait_ge(group_loaded[sg], DMA * LOADS * (b + (g + ahead) // NG + 1))
                                bank_free(count)
                                score(sg, sh, i, half, bank).then_inc(s_filled, 1)
                            elif kind == "turn":
                                turn_sums(n - 1, v, bank, count)
                            else:
                                turn_max((g + 1) % 2, bank, count, n + 1)
                            k += 1
                        u = n * 32 + step
                        if step == 0:
                            pe.wait_ge(max_loaded, DMA * PARTS * (n + 1))
                        if not (first and step < 2):
                            pe.wait_ge(exp_done, u - 1)
                        for half in range(2):
                            last = pe.matmul(m.psT[:, step % 2, half * CHUNK:(half + 1) * CHUNK],
                                             m.kx[:, g, hh, j * P:(j + 1) * P],
                                             m.qx[:, g, hh, half * CHUNK:(half + 1) * CHUNK], start=True, stop=True)
                        last.then_inc(t_filled, 1)
                        if jj == 0 and hh in (1, 3) and not first:
                            weigh(n - 1, (g - 1) % NG, NT - 1, hh // 2, False)
                        for tile, half in plan.get((jj, hh), ()):
                            weigh(n, g, tile, half, first)

            count = 0
            for grp, hh, i in [(0, hh, i) for hh in range(GH) for i in range(NT)] + [(1, 0, i) for i in range(NT)]:
                if hh == 0 and i == 0:
                    pe.wait_ge(group_loaded[grp], DMA * LOADS)
                for half in range(2):
                    bank_free(count)
                    score(grp, hh, i, half, count % 2).then_inc(s_filled, 1)
                    count += 1
                if count == 64:
                    turn_max(0, 0, 64, 0)
                    count += 1
            body(0, 0, 9, first=True)
            with pe.Fori(0, B - 1) as b:
                for g in (1, 2, 3):
                    body(b, g, 9)
                body(b + 1, 0, 9)
            for g in (1, 2, 3):
                body(B - 1, g, NG - g)
            for half in range(2):
                weigh(n_groups - 1, NG - 1, NT - 1, half, False)
            for half in range(2):
                turn_sums(n_groups - 1, half, (parity_end() + half) % 2, s_end() + half)


def project_out(nc, m):
    with ExitStack() as ctx:
        def sem(name):
            return ctx.enter_context(nc.semaphore(f"out_{name}"))

        copied, turned, at_done = sem("copied"), sem("turned"), sem("at_done")
        mixed, biased, added = sem("mixed"), sem("biased"), sem("added")
        block = ctx.enter_context(nc.Block())

        @block.vector
        def _(dve):
            dve.tensor_copy(m.xn[:, 0, :], m.attn[:, chunk_cols(0)]).then_inc(copied, 1)

            def body(chunk, h, more):
                if more:
                    dve.tensor_copy(m.xn[:, 1 - h, :], m.attn[:, chunk_cols(chunk + 1)]).then_inc(copied, 1)
                dve.wait_ge(mixed, chunk + 1)
                bias = m.b_out[:, :].unsqueeze(1).to_broadcast([P, CT, D])
                out = m.psT[:, h, 0:CHUNK].rearrange("p (t d) -> p t d", t=CT)
                mix = m.probs[:, 0, h, 0:CHUNK]
                dve.tensor_tensor(mix.rearrange("p (t d) -> p t d", t=CT), out, bias, ALU.add).then_inc(biased, 1)
                dve.wait_ge(biased, chunk + 1)
                x = m.x[:, chunk_cols(chunk)]
                dve.tensor_tensor(x, x, mix, ALU.add).then_inc(added, 1)

            over_chunks(dve, body)

        @block.scalar
        def _(act):
            def body(chunk, h, more):
                act.wait_ge(turned, chunk + 1)
                act.activation(m.xt[:, h, :], m.psS[:, h, :], ACT.Copy).then_inc(at_done, 1)

            over_chunks(act, body)

        @block.tensor
        def _(pe):
            def body(chunk, h, more):
                pe.wait_ge(copied, chunk + 1)
                for t in range(CT):
                    last = pe.transpose(m.psS[:, h, t * P:(t + 1) * P], m.xn[:, h, t * P:(t + 1) * P], m.ident[:, :])
                last.then_inc(turned, 1)
                pe.wait_ge(at_done, chunk + 1)
                for t in range(CT):
                    last = pe.matmul(m.psT[:, h, t * D:(t + 1) * D], m.xt[:, h, t * P:(t + 1) * P], m.w_out[:, :],
                                     start=True, stop=True, skip_group_check=True)
                last.then_inc(mixed, 1)

            over_chunks(pe, body)


def route(nc, m, xt_all, layer):
    with ExitStack() as ctx:
        def sem(name):
            return ctx.enter_context(nc.semaphore(f"{layer}r_{name}"))

        s = norm_semaphores(nc, ctx, f"{layer}r")
        kept = sem("kept")
        scored, taken = sem("scored"), sem("taken")
        step, exped, ranked = sem("step"), sem("exped"), sem("ranked")
        room = m.room[:, B * S:]

        def scratch(n):
            return room[:, n * TILES * E:(n + 1) * TILES * E].rearrange("p (t e) -> p t e", e=E)

        logits, prob, sel, eq, rank, hot, sel2, hot2 = (scratch(n) for n in range(8))
        small = room[:, 8 * TILES * E:8 * TILES * E + 4 * TILES].rearrange("p (k t) -> p k t", k=4)
        block = ctx.enter_context(nc.Block())

        @block.gpsimd
        def _(pool):
            for e in range(E):
                pool.memset(rank[:, :, e:e + 1], float(E - e)).then_inc(ranked, 1)
            norm_pool_rstd(nc, pool, m, s, 0, 0)

            def body(chunk, h, more):
                if more:
                    norm_pool_rstd(nc, pool, m, s, chunk + 1, 1 - h)

            over_chunks(pool, body)

        @block.scalar
        def _(act):
            def body(chunk, h, more):
                act.wait_ge(s.turned, chunk + 1)
                act.activation(m.xt[:, h, :], m.psS[:, h, :], ACT.Copy).then_inc(s.xt_done, 1)
                act.activation(xt_all[:, chunk_cols(chunk)], m.psS[:, h, :], ACT.Copy).then_inc(kept, 1)

            over_chunks(act, body)
            act.wait_ge(step, 2)
            act.activation(prob, prob, ACT.Exp).then_inc(exped, 1)

        @block.tensor
        def _(pe):
            def body(chunk, h, more):
                norm_pe_turn(nc, pe, m, s, chunk, h)
                pe.wait_ge(s.xt_done, chunk + 1)
                for t in range(CT):
                    last = pe.matmul(m.psO[:, h, t * E:(t + 1) * E], m.xt[:, h, t * P:(t + 1) * P],
                                     m.w_router[:, :], start=True, stop=True, skip_group_check=True)
                last.then_inc(scored, 1)

            over_chunks(pe, body)

        @block.vector
        def _(dve):
            norm_dve_moments(nc, dve, m, s, 0, 0)
            norm_dve_apply(nc, dve, m, s, 0, 0)
            flat = room[:, 0:TILES * E]

            def body(chunk, h, more):
                if more:
                    norm_dve_moments(nc, dve, m, s, chunk + 1, 1 - h)
                    norm_dve_apply(nc, dve, m, s, chunk + 1, 1 - h)
                dve.wait_ge(scored, chunk + 1)
                dve.tensor_copy(flat[:, bass.ds(chunk * (CT * E), CT * E)], m.psO[:, h, 0:CT * E]).then_inc(taken, 1)

            over_chunks(dve, body)

            def wide(k):
                return small[:, k, :].unsqueeze(2).to_broadcast([P, TILES, E])

            done = [0]

            def chain(ins):
                done[0] += 1
                ins.then_inc(step, 1)
                dve.wait_ge(step, done[0])

            dve.wait_ge(taken, 2 * B)
            chain(dve.tensor_reduce(small[:, 0, :], logits, AX.X, ALU.max))
            chain(dve.tensor_tensor(prob, logits, wide(0), ALU.subtract))
            dve.wait_ge(exped, 1)
            chain(dve.tensor_reduce(small[:, 1, :], prob, AX.X, ALU.add))
            chain(dve.reciprocal(small[:, 1, :], small[:, 1, :]))
            chain(dve.tensor_tensor(prob, prob, wide(1), ALU.mult))
            bias = m.e_bias[:, :].unsqueeze(1).to_broadcast([P, TILES, E])
            chain(dve.tensor_tensor(sel, prob, bias, ALU.add))
            dve.wait_ge(ranked, E)
            for src, out in ((sel, hot), (sel2, hot2)):
                chain(dve.tensor_reduce(small[:, 2, :], src, AX.X, ALU.max))
                chain(dve.tensor_tensor(eq, src, wide(2), ALU.is_equal))
                chain(dve.tensor_tensor(eq, eq, rank, ALU.mult))
                chain(dve.tensor_reduce(small[:, 3, :], eq, AX.X, ALU.max))
                chain(dve.tensor_tensor(out, rank, wide(3), ALU.is_equal))
                if out is hot:
                    chain(dve.scalar_tensor_tensor(sel2, hot, -3.0e38, sel, ALU.mult, ALU.add))
            chain(dve.tensor_tensor(hot, hot, hot2, ALU.add))
            chain(dve.tensor_tensor(m.gates[:, :, 0:E], hot, prob, ALU.mult))


def experts(nc, m, xt_all, layer, out):
    last_layer = out is not None
    with ExitStack() as ctx:
        def sem(name):
            return ctx.enter_context(nc.semaphore(f"{layer}e_{name}"))

        h_done = sem("h_done")
        s_done = sem("s_done")
        a_done = sem("a_done")
        y_done = sem("y_done")
        acc_done = sem("acc_done")
        begun = sem("begun")
        passed = sem("passed")
        put = sem("put")
        stored = [sem(f"stored{h}") for h in range(2)]
        acc_free = sem("acc_free")
        room = m.room[:, 2 * B * S:]
        silu = room[:, 0:1024].rearrange("p (k n) -> p k n", k=2)
        hid = room[:, 1024:2048].rearrange("p (k n) -> p k n", k=2)
        acc = room[:, 2048:3072].rearrange("p (k n) -> p k n", k=2)
        gate = room[:, 3072:3072 + 2 * CT * NE].rearrange("p (k t e) -> p k t e", k=2, t=CT)
        block = ctx.enter_context(nc.Block())
        gates_flat = m.gates[:, :, :].rearrange("p t e -> p (t e)")

        @block.tensor
        def _(pe):
            def hidden(b, k):
                h, e = divmod(k, NE)
                x1 = xt_all[:, bass.ds((b * 2 + h) * CHUNK, CHUNK)]
                pe.matmul(m.psT[:, k % 2, 0:CHUNK], m.w1[:, e, :], x1, start=True, stop=True)
                pe.matmul(m.psT[:, k % 2, CHUNK:2 * CHUNK], m.w3[:, e, :], x1, start=True, stop=True
                          ).then_inc(h_done, 1)

            def output(b, k):
                e = k % NE
                pe.wait_ge(a_done, b * (2 * NE) + k + 1)
                if k >= 2:
                    pe.wait_ge(acc_done, (b * (2 * NE) + k - 1) * CT)
                for t in range(CT):
                    last = pe.matmul(m.psS[:, k % 2, t * D:(t + 1) * D], hid[:, k % 2, t * P:(t + 1) * P],
                                     m.w2[:, e, :], start=True, stop=True, skip_group_check=True)
                last.then_inc(y_done, 1)

            with pe.Fori(0, B) as b:
                hidden(b, 0)
                for k in range(2 * NE):
                    if k + 1 < 2 * NE:
                        hidden(b, k + 1)
                    output(b, k)
                pe.wait_ge(acc_done, (b + 1) * (2 * NE * CT))

        @block.scalar
        def _(act):
            with act.Fori(0, B) as b:
                for k in range(2 * NE):
                    act.wait_ge(h_done, b * (2 * NE) + k + 1)
                    act.activation(silu[:, k % 2, :], m.psT[:, k % 2, 0:CHUNK], ACT.Silu).then_inc(s_done, 1)

        @block.vector
        def _(dve):
            def begin(b, h):
                chunk = b * 2 + h
                if last_layer:
                    dve.wait_ge(acc_free, chunk + 1)
                dve.tensor_copy(acc[:, h, :], m.x[:, chunk_cols(chunk)]).then_inc(begun, 1)
                dve.tensor_copy(gate[:, h, :, :].rearrange("p t e -> p (t e)"),
                                gates_flat[:, bass.ds(chunk * (CT * NE), CT * NE)]).then_inc(begun, 1)

            def gather(b, k):
                h, e = divmod(k, NE)
                before = (b * (2 * NE) + k) * CT
                dve.wait_ge(y_done, b * (2 * NE) + k + 1)
                if e == 0:
                    dve.wait_ge(begun, (b * 2 + h) * 2 + 2)
                else:
                    dve.wait_ge(acc_done, before)
                for t in range(CT):
                    part = acc[:, h, t * D:(t + 1) * D]
                    dve.scalar_tensor_tensor(part, m.psS[:, k % 2, t * D:(t + 1) * D], gate[:, h, t, e:e + 1],
                                             part, ALU.mult, ALU.add).then_inc(acc_done, 1)
                if e == NE - 1:
                    hold(dve, acc_done, before + CT, passed)
                    if not last_layer:
                        dve.tensor_copy(m.x[:, chunk_cols(b * 2 + h)], acc[:, h, :]).then_inc(put, 1)

            with dve.Fori(0, B) as b:
                for k in range(2 * NE):
                    if k % NE == 0:
                        begin(b, k // NE)
                    dve.wait_ge(s_done, b * (2 * NE) + k + 1)
                    dve.tensor_tensor(hid[:, k % 2, :], silu[:, k % 2, :], m.psT[:, k % 2, CHUNK:2 * CHUNK],
                                      ALU.mult).then_inc(a_done, 1)
                    if k:
                        gather(b, k - 1)
                gather(b, 2 * NE - 1)

        if last_layer:
            @block.sync
            def _(sp):
                sp.sem_inc(acc_free, 2)
                rows = out.rearrange("b (h t p) d -> p b h t d", p=P, t=CT)
                with sp.Fori(0, B) as b:
                    for h in range(2):
                        sp.wait_ge(acc_done, (b * (2 * NE) + (h + 1) * NE) * CT)
                        sp.dma_start(rows[:, bass.ds(b, 1), h, :, :].rearrange("p b t d -> p (b t) d"),
                                     acc[:, h, :].rearrange("p (t d) -> p t d", t=CT)).then_inc(stored[h], DMA)
                        sp.wait_ge(stored[h], DMA * (b + 1))
                        sp.sem_inc(acc_free, 1)


def build(nc, a, out):
    with ExitStack() as ctx:
        m = allocate(nc, ctx)
        xt_all = m.room[:, 0:B * S]
        setup(nc, m, a)
        project(nc, m, "a", [])
        attend(nc, m, "a")
        route(nc, m, xt_all, "a")
        experts(nc, m, xt_all, "a", None)
        project(nc, m, "b", [
            (m.w_q[:, 0, 0, :], a["b_wq"]), (m.w_q[:, 1, 0, :], a["b_wk"]),
            (m.w_q[:, 0, 1, :], a["b_wq_swapped"]), (m.w_q[:, 1, 1, :], a["b_wk_swapped"]),
            (m.w_v[:, :], a["b_wv"]), (m.rope, a["rope"]),
        ])
        attend(nc, m, "b")
        project_out(nc, m)
        route(nc, m, xt_all, "b")
        experts(nc, m, xt_all, "b", out)




def _layout(i):
    perm = np.arange(D).reshape(NG, GH, HD).transpose(0, 2, 1).reshape(-1)
    swap = np.roll(np.arange(D).reshape(NG, GH, HD), HD // 2, axis=2).transpose(0, 2, 1).reshape(-1)
    qkv = np.asarray(i["L0_attn_b_w_qkv"]).T
    wq, wk, wv = qkv[:, 0:D], qkv[:, D:2 * D], qkv[:, 2 * D:3 * D]
    return {
        "x": i["L0_attn_a_content"],
        "a_wq": i["L0_attn_a_Wq"][:, perm], "a_wk": i["L0_attn_a_Wk"][:, perm], "a_wv": i["L0_attn_a_Wv"][:, perm],
        "b_wq": wq[:, perm], "b_wk": wk[:, perm], "b_wv": wv[:, perm],
        "b_wq_swapped": wq[:, swap], "b_wk_swapped": wk[:, swap],
        "b_wout": np.asarray(i["L0_attn_b_w_out"]).T, "b_bias": i["L0_attn_b_b_out"],
        "router": i["L0_ffn_router_w"], "e_bias": i["L0_ffn_expert_bias"],
        "w1": i["L0_ffn_w1"], "w2": i["L0_ffn_w2"], "w3": i["L0_ffn_w3"],
        "sw1": i["L0_ffn_sw1"], "sw2": i["L0_ffn_sw2"], "sw3": i["L0_ffn_sw3"],
    }


def _rope_tables():
    half = HD // 2
    inv = (1.0 / 10000.0 ** (np.arange(0, HD, 2, dtype=np.float32) / np.float32(HD))).astype(np.float32)
    angle = (np.arange(S, dtype=np.float32)[:, None] * inv[None, :]).astype(np.float32).astype(np.float64)
    cos, sin = np.cos(angle).T, np.sin(angle).T
    rows = np.stack([np.concatenate([cos, cos]), np.concatenate([-sin, sin])])
    rows = np.broadcast_to(rows[:, None, :, None, :], (2, NG, 2 * half, GH, S)).reshape(2, P, S)
    return np.ascontiguousarray(rows.transpose(1, 0, 2)).astype(np.float32)


def kernel(**inputs):
    import concourse.bacc as bacc
    from concourse.bass_utils import run_bass_kernel_spmd

    nc = bacc.Bacc("TRN2", target_bir_lowering=False, num_devices=1)
    arrays = {f"in_{k}": np.ascontiguousarray(v) for k, v in _layout({k: np.asarray(v) for k, v in inputs.items()}).items()}
    arrays["in_rope"] = _rope_tables()
    args = {k[3:]: nc.dram_tensor(k, v.shape, F32, kind="ExternalInput").ap() for k, v in arrays.items()}
    out = nc.dram_tensor("out_dram", (B, S, D), F32, kind="ExternalOutput").ap()
    build(nc, args, out)
    r = run_bass_kernel_spmd(nc, [arrays], core_ids=[0])
    return r.results[0]["out_dram"]
```

```python
from contextlib import ExitStack

import numpy as np

import concourse.bass as bass
from concourse import mybir

F32 = mybir.dt.float32
BF16 = mybir.dt.bfloat16
F32R = mybir.dt.float32r
ALU = mybir.AluOpType
ACT = mybir.ActivationFunctionType
AX = mybir.AxisListType

P = 128
B = 4
S = 1024
D = 128
HD = 8
NG = 4
GH = 4
GR = GH * HD
NT = S // P
TILES = B * NT
CHUNK = 512
CT = CHUNK // P
CHUNKS = B * S // CHUNK
HALVES = S // CHUNK
E = 8
NE = E + 1
PARTS = 3
PR = 32
MAXROW = PARTS * PR
VW = (HD + 1) * GH
EPS = 1e-5
SCALE = float(HD) ** -0.5
DMA = 16


class Buffers:
    pass


def allocate(nc, ctx):
    m = Buffers()

    def sb(name, shape, dt=F32):
        return ctx.enter_context(nc.sbuf_tensor(name, shape, dt))

    m.x = sb("x", [P, TILES * D])
    m.attn = sb("attn", [P, TILES * D])
    m.ident = sb("ident", [P, P])
    m.w_q = sb("w_q", [P, 2, 2, D])
    m.w_v = sb("w_v", [P, D])
    m.w_out = sb("w_out", [P, D])
    m.b_out = sb("b_out", [P, D])
    m.rope = m.attn[:, 0:2 * S].rearrange("p (k s) -> p k s", k=2)
    m.w_router = sb("w_router", [P, E])
    m.e_bias = sb("e_bias", [P, E])
    m.w1 = sb("w1", [P, NE, D])
    m.w2 = sb("w2", [P, NE, D])
    m.w3 = sb("w3", [P, NE, D])
    m.gates = sb("gates", [P, TILES, NE])
    m.xn = sb("xn", [P, 2, CHUNK])
    m.xt = sb("xt", [P, 2, CHUNK])
    m.stats = sb("stats", [P, 2, CT, 6])
    m.mv = sb("mv", [P, 2, CT, 2])
    m.shifted = sb("shifted", [P, 2, CT])
    m.mean = sb("mean", [P, TILES])
    m.rstd = sb("rstd", [P, TILES])
    m.expo = sb("expo", [P, CT])
    m.qx = sb("qx", [P, NG, GH, S], BF16)
    m.kx = sb("kx", [P, NG, GH, S], BF16)
    m.vg = sb("vg", [P, NG, NT, VW])
    m.causal = sb("causal", [P, P])
    m.w01 = sb("w01", [P, HD + 1])
    m.ps_one = ctx.enter_context(nc.psum_tensor("ps_one", [P, 2, CHUNK], F32))
    m.ps_two = ctx.enter_context(nc.psum_tensor("ps_two", [P, 2, 2 * CHUNK], F32))
    m.ps_sum = ctx.enter_context(nc.psum_tensor("ps_sum", [P, 2, CHUNK], F32))
    m.qk_parts = nc.dram_tensor("qk_parts", (B, PARTS, 2, P, S), BF16, kind="Internal").ap()
    m.v_rows = nc.dram_tensor("v_rows", (B, NT, P, D), F32, kind="Internal").ap()
    m.passed_dve, m.passed_pool = (ctx.enter_context(nc.semaphore(name)) for name in ("passed_dve", "passed_pool"))
    return m


def tile_cols(tile):
    return bass.ds(tile * D, D)


def chunk_cols(chunk):
    return bass.ds(chunk * CHUNK, CHUNK)


def hold(eng, sem, value, passed):
    eng.wait_ge(sem, value)
    eng.sem_inc(passed, 1)


def over_chunks(eng, body, lead=0, start=0):
    pairs = (CHUNKS - lead - start) // 2

    def run(t, low, high):
        body(t, low, lambda k: low + k >= 0 and high + k < CHUNKS)

    for t in range(-lead, start):
        run(t, t, t)
    with eng.Fori(0, pairs) as i:
        for h in range(2):
            run(i * 2 + (start + h), start + h, start + h + 2 * pairs - 2)
    for t in range(start + 2 * pairs, CHUNKS):
        run(t, t, t)


def moment_semaphores(nc, ctx, tag):
    def sem(name):
        return ctx.enter_context(nc.semaphore(f"{tag}_{name}"))

    s = Buffers()
    s.moments = sem("moments")
    s.stats_done = sem("stats_done")
    s.stats_kept = sem("stats_kept")
    s.shifted = sem("shifted")
    s.rstd_done = sem("rstd_done")
    return s


def moments(dve, m, s, chunk, h):
    hold(dve, s.rstd_done, chunk + 1, m.passed_dve)
    for t in range(CT):
        dve.bn_stats(m.stats[:, h, t, :], m.x[:, tile_cols(chunk * CT + t)]).then_inc(s.moments, 1)
    hold(dve, s.moments, chunk * CT + CT, m.passed_dve)
    for t in range(CT):
        dve.bn_aggr(m.mv[:, h, t, :], m.stats[:, h, t, :]).then_inc(s.stats_done, 1)
    hold(dve, s.stats_done, chunk * CT + CT, m.passed_dve)
    dve.tensor_copy(m.mean[:, bass.ds(chunk * CT, CT)], m.mv[:, h, :, 0]).then_inc(s.stats_kept, 1)


def deviations(pool, m, s, chunk, h):
    hold(pool, s.stats_kept, chunk + 1, m.passed_pool)
    pool.tensor_scalar(m.shifted[:, h, :], m.mv[:, h, :, 1], EPS, 0.0, ALU.add, ALU.add).then_inc(s.shifted, 1)
    hold(pool, s.shifted, chunk + 1, m.passed_pool)
    pool.tensor_tensor(m.rstd[:, bass.ds(chunk * CT, CT)], m.shifted[:, h, :], m.expo[:, :],
                       ALU.pow).then_inc(s.rstd_done, 1)


def setup(nc, m, a):
    with ExitStack() as ctx:
        x_loaded = [ctx.enter_context(nc.semaphore(f"x_loaded{b}")) for b in range(B)]
        loaded = ctx.enter_context(nc.semaphore("loaded"))
        cleared = ctx.enter_context(nc.semaphore("cleared"))
        s = moment_semaphores(nc, ctx, "s")
        block = ctx.enter_context(nc.Block())
        loads = [
            (m.w_q[:, 0, 0, :], a["a_wq"]),
            (m.w_q[:, 1, 0, :], a["a_wk"]),
            (m.w_v[:, :], a["a_wv"]),
        ]

        @block.sync
        def _(sp):
            for b in range(B):
                sp.dma_start(m.x[:, b * NT * D:(b + 1) * NT * D].rearrange("p (t d) -> p t d", d=D),
                             a["x"][b, :, :].rearrange("(t p) d -> p t d", p=P)).then_inc(x_loaded[b], DMA)
            for out, src in loads:
                sp.dma_start(out, src).then_inc(loaded, DMA)
            sp.wait_ge(loaded, DMA * len(loads))

        @block.gpsimd
        def _(pool):
            pool.memset(m.kx[:, :, :, :].bitcast(F32), 0.0).then_inc(cleared, 1)
            pool.memset(m.ident[:, :], 0.0).then_inc(cleared, 1)
            pool.memset(m.w01[:, :], 0.0).then_inc(cleared, 1)
            pool.memset(m.causal[:, :], 1.0).then_inc(cleared, 1)
            pool.memset(m.expo[:, :], -0.5)
            pool.memset(m.vg[:, :, :, GR:VW], 1.0)
            pool.memset(m.gates[:, :, E:NE], 1.0)
            pool.wait_ge(cleared, 4)
            pool.affine_select(out=m.causal[:, :], in_=m.causal[:, :], compare_op=ALU.is_ge, fill=0.0,
                               base=0, pattern=[[1, P]], channel_multiplier=-1)
            pool.affine_select(out=m.ident[:, :], in_=m.ident[:, :], compare_op=ALU.not_equal, fill=1.0,
                               base=0, pattern=[[-1, P]], channel_multiplier=1)
            pool.memset(m.w01[:, HD:HD + 1], 1.0)
            pool.sem_inc(s.rstd_done, 2)
            for chunk in range(CHUNKS):
                deviations(pool, m, s, chunk, chunk % 2)

        @block.vector
        def _(dve):
            for chunk in range(CHUNKS):
                dve.wait_ge(x_loaded[chunk // HALVES], DMA)
                moments(dve, m, s, chunk, chunk % 2)


def norm_semaphores(nc, ctx, tag):
    def sem(name):
        return ctx.enter_context(nc.semaphore(f"{tag}_{name}"))

    s = Buffers()
    s.xn_done = sem("xn_done")
    s.turned = sem("turned")
    s.xt_done = sem("xt_done")
    return s


def norm_dve_apply(dve, m, s, chunk, low):
    if low >= 2:
        dve.wait_ge(s.turned, chunk - 1)
    for t in range(CT):
        tile = chunk * CT + t
        dve.tensor_scalar(m.xn[:, low % 2, t * P:(t + 1) * P], m.x[:, tile_cols(tile)],
                          m.mean[:, bass.ds(tile, 1)], m.rstd[:, bass.ds(tile, 1)],
                          ALU.subtract, ALU.mult).then_inc(s.xn_done, 1)


def norm_pe_turn(pe, m, s, chunk, low):
    h = low % 2
    pe.wait_ge(s.xn_done, chunk * CT + CT)
    if low >= 2:
        pe.wait_ge(s.xt_done, chunk - 1)
    for t in range(CT):
        last = pe.transpose(m.ps_one[:, h, t * P:(t + 1) * P], m.xn[:, h, t * P:(t + 1) * P], m.ident[:, :])
    last.then_inc(s.turned, 1)


LOADS = 2 * PARTS + 1


def load_group(sp, m, b, g, group_loaded):
    for p in range(PARTS):
        rows = slice(p * PR, p * PR + PARTS * HD)
        for c, (dst, first_part, parts) in enumerate(((m.qx, p, 1), (m.kx, 0, PARTS))):
            src = m.qk_parts[bass.ds(b, 1), first_part:first_part + parts, c, g * GR:(g + 1) * GR, :]
            src = src.rearrange("b c (d h) s -> (b c) d (h s)", h=GH)
            sp.dma_start(dst[rows, g, :, :].rearrange("p h s -> p (h s)"),
                         src.to_broadcast([PARTS, HD, GH * S])).then_inc(group_loaded[g], DMA)
    sp.dma_start(m.vg[:, g, :, 0:GR],
                 m.v_rows[bass.ds(b, 1), :, :, g * GR:(g + 1) * GR].rearrange("b t p r -> p (b t) r")
                 ).then_inc(group_loaded[g], DMA)


def project(nc, m, layer, later, group_loaded):
    rope = layer == "b"
    with ExitStack() as ctx:
        def sem(name):
            return ctx.enter_context(nc.semaphore(f"{layer}p_{name}"))

        def sb(name, shape, dt=F32):
            return ctx.enter_context(nc.sbuf_tensor(f"{layer}p_{name}", shape, dt))

        s = norm_semaphores(nc, ctx, f"{layer}p")
        later_loaded = sem("later_loaded")
        qk_done = sem("qk_done")
        v_done = sem("v_done")
        v_copied = sem("v_copied")
        product = sem("product")
        rotated = sem("rotated")
        high = sem("high")
        rest1 = sem("rest1")
        middle = sem("middle")
        low_done = sem("low_done")
        zeroed = sem("zeroed")
        ones_set = sem("ones_set")
        first_stored = sem("first_stored")
        others_stored = sem("others_stored")
        v_stored = [sem(f"v_stored{h}") for h in range(2)]
        v_free = sem("v_free")
        pbuf = sb("parts", [P, CHUNKS * PARTS, 2 * CHUNK], BF16)
        vbuf = sb("vbuf", [P, 2, CHUNK])
        rest = sb("rest", [P, 2, 2 * CHUNK])
        prod_c = sb("prod_c", [P, 2, 2 * CHUNK])
        prod_s = sb("prod_s", [P, 2 * CHUNK])[:, :]
        USES = 2 if rope else 1

        def source(h):
            return prod_c[:, h, :] if rope else m.ps_two[:, h, :]

        def part(chunk, c):
            return pbuf[:, bass.ds(chunk * PARTS + c, 1), :].rearrange("p u n -> p (u n)")

        block = ctx.enter_context(nc.Block())

        @block.sync
        def _(sp):
            for out, src in later:
                sp.dma_start(out, src).then_inc(later_loaded, DMA)
            sp.sem_inc(v_free, 2)

            def store(b, h, parts_stored):
                chunk = b * 2 + h
                sp.wait_ge(v_copied, chunk + 1)
                tokens = m.v_rows[bass.ds(b, 1), h * CT:(h + 1) * CT, :, :].rearrange("b t p r -> p (b t) r")
                sp.dma_start(tokens, vbuf[:, h, :].rearrange("p (t r) -> p t r", t=CT)).then_inc(v_stored[h], DMA)
                for c, part_done in enumerate((high, middle, low_done)):
                    if c == PARTS - 1:
                        sp.wait_ge(v_stored[h], (b + 1) * DMA)
                        sp.sem_inc(v_free, 1)
                    sp.wait_ge(part_done, chunk + 1)
                    rows = m.qk_parts[bass.ds(b, 1), c, :, :, h * CHUNK:(h + 1) * CHUNK]
                    sp.dma_start(rows.rearrange("b i p n -> p (b i) n"),
                                 part(chunk, c).rearrange("p (i n) -> p i n", i=2)).then_inc(parts_stored, DMA)

            for h in range(2):
                store(0, h, first_stored)
            with sp.Fori(0, B - 2) as b:
                for h in range(2):
                    store(b + 1, h, others_stored)
            if not rope:
                sp.wait_ge(zeroed, NG)
            sp.wait_ge(first_stored, DMA * PARTS * HALVES)
            load_group(sp, m, 0, 0, group_loaded)
            for h in range(2):
                store(B - 1, h, others_stored)
            sp.wait_ge(others_stored, DMA * PARTS * (CHUNKS - HALVES))
            if later:
                sp.wait_ge(later_loaded, DMA * len(later))

        @block.gpsimd
        def _(pool):
            if not rope:
                pool.memset(m.kx[MAXROW:MAXROW + PARTS, :, :, :], 1.0).then_inc(ones_set, 1)
                pool.wait_ge(ones_set, 1)

            def body(t, low, has):
                if rope and has(2):
                    chunk, h = t + 2, low % 2
                    pool.wait_ge(product, chunk * 2 + 2)
                    pool.tensor_tensor(prod_c[:, h, :], prod_c[:, h, :], prod_s, ALU.add
                                       ).then_inc(rotated, 1)
                if has(0):
                    h = low % 2
                    hold(pool, middle, t + 1, m.passed_pool)
                    pool.tensor_tensor(part(t, 2), rest[:, h, :], part(t, 1), ALU.subtract
                                       ).then_inc(low_done, 1)

            over_chunks(pool, body, lead=2)

        @block.vector
        def _(dve):
            def body(t, low, has):
                if has(3):
                    norm_dve_apply(dve, m, s, t + 3, low + 3)
                if not rope and low == -1:
                    for g in range(NG):
                        dve.memset(m.qx[:, g, :, :].bitcast(F32), 0.0).then_inc(zeroed, 1)
                if rope and has(1):
                    chunk, h = t + 1, (low + 1) % 2
                    if low + 1 >= 2:
                        dve.wait_ge(rest1, chunk - 1)
                    for n in range(2):
                        if n and low + 1 >= 1:
                            dve.wait_ge(rotated, chunk)
                        dve.wait_ge(qk_done, chunk * 2 + n + 1)
                        half = low + 1 & 1
                        table = m.rope[:, n, half * CHUNK:(half + 1) * CHUNK].unsqueeze(1).to_broadcast([P, 2, CHUNK])
                        dve.tensor_tensor((prod_s if n else prod_c[:, h, :]).rearrange("p (i n) -> p i n", i=2),
                                          m.ps_two[:, n, :].rearrange("p (i n) -> p i n", i=2), table,
                                          ALU.mult).then_inc(product, 1)
                if has(0):
                    h = low % 2
                    dve.wait_ge(high, t + 1)
                    if low >= 2:
                        dve.wait_ge(low_done, t - 1)
                    dve.tensor_tensor(rest[:, h, :], source(h), part(t, 0), ALU.subtract).then_inc(rest1, 1)

            over_chunks(dve, body, lead=3, start=2)

        @block.scalar
        def _(act):
            def body(t, low, has):
                if has(3):
                    h = (low + 3) % 2
                    act.wait_ge(s.turned, t + 4)
                    act.activation(m.xt[:, h, :], m.ps_one[:, h, :], ACT.Copy).then_inc(s.xt_done, 1)
                if has(1):
                    chunk, h = t + 1, (low + 1) % 2
                    act.wait_ge(v_free, chunk + 1)
                    act.wait_ge(v_done, chunk + 1)
                    act.activation(vbuf[:, h, :], m.ps_sum[:, h, :], ACT.Copy).then_inc(v_copied, 1)
                    if rope:
                        act.wait_ge(rotated, chunk + 1)
                    else:
                        act.wait_ge(qk_done, chunk + 1)
                    act.activation(part(chunk, 0), source(h), ACT.Copy).then_inc(high, 1)
                if has(0):
                    h = low % 2
                    act.wait_ge(rest1, t + 1)
                    act.activation(part(t, 1), rest[:, h, :], ACT.Copy).then_inc(middle, 1)

            over_chunks(act, body, lead=3)

        @block.tensor
        def _(pe):
            def body(t, low, has):
                if has(1):
                    norm_pe_turn(pe, m, s, t + 1, low + 1)
                if has(0):
                    h = low % 2
                    pe.wait_ge(s.xt_done, t + 1)
                    for n in range(USES):
                        slot = n if rope else h
                        if rope and low >= 1:
                            pe.wait_ge(product, t * 2 + n - 1)
                        if not rope and low >= 2:
                            pe.wait_ge(rest1, t - 1)
                        for i in range(2):
                            last = pe.matmul(m.ps_two[:, slot, i * CHUNK:(i + 1) * CHUNK],
                                             m.w_q[:, i, n, :], m.xt[:, h, :], start=True, stop=True)
                        last.then_inc(qk_done, 1)
                    if low >= 2:
                        pe.wait_ge(v_copied, t - 1)
                    for k in range(CT):
                        last = pe.matmul(m.ps_sum[:, h, k * D:(k + 1) * D], m.xt[:, h, k * P:(k + 1) * P],
                                         m.w_v[:, :], start=True, stop=True, skip_group_check=True)
                    last.then_inc(v_done, 1)

            over_chunks(pe, body, lead=1, start=2)


def attend(nc, m, layer, group_loaded):
    masked_after = layer == "a"
    n_groups = B * NG
    order = list(range(NT - 1, -1, -1))
    STEPS = NT * GH
    QUARTER = S // 4
    USES = STEPS + 2
    AHEAD = STEPS + 1
    with ExitStack() as ctx:
        def sem(name):
            return ctx.enter_context(nc.semaphore(f"{layer}t_{name}"))

        def sb(name, shape, dt=F32):
            return ctx.enter_context(nc.sbuf_tensor(f"{layer}t_{name}", shape, dt))

        two_filled = sem("two_filled")
        two_read = sem("two_read")
        split = sem("split")
        max_loaded = sem("max_loaded")
        t_filled = sem("t_filled")
        exp_done = sem("exp_done")
        masked = sem("masked")
        pv_done = sem("pv_done")
        o_copied = sem("o_copied")
        o_step = sem("o_step")
        mom = moment_semaphores(nc, ctx, f"{layer}tm") if masked_after else None
        probs = sb("probs", [P, 4, GH, S])
        negmax = sb("negmax", [P, 2, STEPS])
        turned_max = sb("turned_max", [STEPS, P])
        left = sb("left", [STEPS, P])
        mparts = sb("mparts", [STEPS, PARTS, P], BF16)
        sums = sb("sums", [P, S])
        recip = sb("recip", [P, NT, GH, 1])
        heads = sb("heads", [P, NT, GH, HD])
        pdiag = sb("pdiag", [P, 2, GH, P])
        block = ctx.enter_context(nc.Block())

        def scores_beside(n_left):
            return STEPS if n_left >= 3 else STEPS - NT if n_left == 2 else 0

        def score_step(v):
            return (1 + (NT + v) // STEPS, (NT + v) // NT % GH, v % NT)

        def uses(n_left, first):
            out = []
            v = -NT if first else 0
            for step in range(STEPS):
                until = (step + 1) * (STEPS + NT) // STEPS - NT if first else min(step + 1, scores_beside(n_left))
                while v < until:
                    out.append((step, "score", v))
                    v += 1
                if step == NT and not first:
                    out.append((step, "sums", 0))
                if step == STEPS - NT + (3 if first else 1) and n_left >= 2:
                    out.append((step, "max", 0))
            return out

        def uses_before(n, n_left, first):
            if first:
                return AHEAD
            return n * USES + AHEAD + NT - 1 - (NT if n_left == 1 else 0)

        def slot_of(g, first):
            return uses_before(g if g else NG, NG, first) % 2

        uses_in_all = uses_before(n_groups - 1, 1, False) + 1

        def over_groups(eng, body):
            body(0, 0, n_groups, True)
            with eng.Fori(0, B - 1) as b:
                for g in range(1, NG):
                    body(b, g, NG, False)
                body(b + 1, 0, NG, False)
            for g in range(1, NG):
                body(B - 1, g, NG - g, False)

        @block.sync
        def _(sp):
            def maxima(n, g):
                sp.wait_ge(split, 4 * n + 4)
                for c in range(PARTS):
                    sp.dma_start(m.qx[MAXROW + c:MAXROW + c + 1, g, :, :].rearrange("p h (t q) -> p (h t) q", q=P),
                                 mparts[:, c, :]).then_inc(max_loaded, DMA)

            def body(b, g, n_left, first):
                n = b * NG + g
                if n_left >= 4:
                    if not first:
                        sp.wait_ge(pv_done, STEPS * n)
                    load_group(sp, m, b + (g + 3) // NG, (g + 3) % NG, group_loaded)
                if n_left >= 2:
                    maxima(n + 1, (g + 1) % NG)

            for g in range(1, 3):
                load_group(sp, m, 0, g, group_loaded)
            maxima(0, 0)
            over_groups(sp, body)

        @block.gpsimd
        def _(pool):
            def split_max(n, count, first=False):
                hold(pool, two_read, count, m.passed_pool)
                if not first:
                    hold(pool, max_loaded, DMA * PARTS * n, m.passed_pool)
                pool.tensor_copy(mparts[:, 0, :], turned_max[:, :]).then_inc(split, 1)
                pool.wait_ge(split, 4 * n + 1)
                pool.tensor_tensor(left[:, :], turned_max[:, :], mparts[:, 0, :], ALU.subtract).then_inc(split, 1)
                hold(pool, split, 4 * n + 2, m.passed_pool)
                pool.tensor_copy(mparts[:, 1, :], left[:, :]).then_inc(split, 1)
                pool.wait_ge(split, 4 * n + 3)
                pool.tensor_tensor(mparts[:, 2, :], left[:, :], mparts[:, 1, :], ALU.subtract).then_inc(split, 1)

            def body(b, g, n_left, first):
                n = b * NG + g
                for jj, j in enumerate(order):
                    if masked_after:
                        pool.wait_ge(exp_done, (n * STEPS + jj * GH + GH) * 2)
                        if not (first and jj < 2):
                            pool.wait_ge(pv_done, n * STEPS + 4 * (jj - 1))
                        pool.tensor_tensor(pdiag[:, jj % 2, :, :], probs[:, jj % 4, :, j * P:(j + 1) * P],
                                           m.causal[:, :].unsqueeze(1).to_broadcast([P, GH, P]),
                                           ALU.mult).then_inc(masked, 1)
                    if masked_after and g == 0 and not first and jj == 4:
                        for h in range(HALVES):
                            deviations(pool, m, mom, (b - 1) * HALVES + h, h)
                    if jj == 5 and n_left >= 2:
                        done = [kind for _, kind, _ in uses(n_left, first)].index("max") + 1
                        split_max(n + 1, uses_before(n, n_left, first) + done)

            if masked_after:
                pool.sem_inc(mom.rstd_done, 2)
            split_max(0, STEPS + 1, first=True)
            over_groups(pool, body)
            if masked_after:
                for h in range(HALVES):
                    deviations(pool, m, mom, (B - 1) * HALVES + h, h)

        @block.scalar
        def _(act):
            def copy_sums(n, half):
                act.wait_ge(pv_done, (n + 1) * STEPS - 2 * (1 - half))
                act.activation(sums[:, half * CHUNK:(half + 1) * CHUNK], m.ps_sum[:, half, :],
                               ACT.Copy).then_inc(o_copied, 1)

            def body(b, g, n_left, first):
                n = b * NG + g
                for jj in range(NT):
                    if not (first and jj < 4):
                        act.wait_ge(pv_done, n * STEPS + 4 * (jj - 3))
                    for hh in range(GH):
                        for half in range(2):
                            act.wait_ge(t_filled, (n * STEPS + jj * GH + hh) * 2 + half + 1)
                            act.activation(probs[:, jj % 4, hh, half * CHUNK:(half + 1) * CHUNK],
                                           m.ps_one[:, half, :], ACT.Exp, scale=SCALE).then_inc(exp_done, 1)
                        if not first and (jj, hh) in ((0, 2), (1, 0)):
                            copy_sums(n - 1, jj)

            over_groups(act, body)
            for half in range(2):
                copy_sums(n_groups - 1, half)

        @block.vector
        def _(dve):
            def take_max(parity, hh, i, slot, count):
                dve.wait_ge(two_filled, count + 1)
                dve.tensor_reduce(negmax[:, parity, hh * NT + i:hh * NT + i + 1], m.ps_two[:, slot, :],
                                  AX.X, ALU.max, negate=True).then_inc(two_read, 1)

            def copy_max(slot, count, n, first=False):
                dve.wait_ge(two_filled, count + 1)
                if not first:
                    dve.wait_ge(split, 4 * n)
                dve.tensor_copy(turned_max[:, :], m.ps_two[0:STEPS, slot, 0:P]).then_inc(two_read, 1)

            def finish(n, b, g, slot, count):
                dve.wait_ge(two_filled, count + 1)
                src = m.ps_two[:, slot, :].rearrange("p (t h r) -> p t h r", t=NT, h=GH)
                dve.reciprocal(recip[:, :, :, :], src[:, :, :, HD:HD + 1]).then_inc(o_step, 1)
                dve.wait_ge(o_step, n * 3 + 1)
                dve.tensor_tensor(heads[:, :, :, :], src[:, :, :, 0:HD],
                                  recip[:, :, :, :].to_broadcast([P, NT, GH, HD]), ALU.mult).then_inc(two_read, 1)
                hold(dve, two_read, count + 1, m.passed_dve)
                dest = m.x if masked_after else m.attn
                cols = dest[:, bass.ds(b * (NT * D), NT * D)]
                cols = cols.rearrange("p (t d) -> p t d", t=NT)[:, :, g * GR:(g + 1) * GR]
                flat = heads[:, :, :, :].rearrange("p t h d -> p t (h d)")
                if masked_after:
                    dve.tensor_tensor(cols, cols, flat, ALU.add).then_inc(o_step, 2)
                else:
                    dve.tensor_copy(cols, flat).then_inc(o_step, 2)

            def sequence_moments(n, b):
                hold(dve, o_step, n * 3, m.passed_dve)
                for h in range(HALVES):
                    moments(dve, m, mom, b * HALVES + h, h)

            def body(b, g, n_left, first):
                n = b * NG + g
                for k, (_, kind, v) in enumerate(uses(n_left, first)):
                    count, slot = uses_before(n, n_left, first) + k, (slot_of(g, first) + k) % 2
                    if kind == "score":
                        ahead, hh, i = score_step(v)
                        take_max((g + ahead) % 2, hh, i, slot, count)
                    elif kind == "sums":
                        finish(n - 1, *((b, g - 1) if g else (b - 1, NG - 1)), slot, count)
                        if masked_after and g == 0:
                            sequence_moments(n, b - 1)
                    else:
                        copy_max(slot, count, n + 1)

            for v in range(STEPS):
                take_max(0, v // NT, v % NT, v % 2, v)
            copy_max(0, STEPS, 0, first=True)
            over_groups(dve, body)
            finish(n_groups - 1, B - 1, NG - 1, uses_in_all % 2, uses_in_all)
            if masked_after:
                sequence_moments(n_groups, B - 1)

        @block.tensor
        def _(pe):
            def slot_free(count, first=False):
                if not first:
                    pe.wait_ge(two_read, count - 1)

            def score(g, hh, i, slot):
                for half in range(2):
                    last = pe.matmul(m.ps_two[:, slot, half * CHUNK:(half + 1) * CHUNK],
                                     m.qx[0:MAXROW, g, hh, i * P:(i + 1) * P],
                                     m.kx[0:MAXROW, g, hh, half * CHUNK:(half + 1) * CHUNK], start=True, stop=True)
                last.then_inc(two_filled, 1)

            def turn_max(parity, slot, count):
                pe.wait_ge(two_read, count)
                pe.transpose(m.ps_two[0:STEPS, slot, 0:P], negmax[:, parity, :], m.ident[:, :]
                             ).then_inc(two_filled, 1)

            def turn_sums(n, slot, count):
                pe.wait_ge(o_copied, 2 * n + 2)
                slot_free(count)
                for t in range(NT):
                    last = pe.transpose(m.ps_two[:, slot, t * P:(t + 1) * P], sums[:, t * P:(t + 1) * P],
                                        m.ident[:, :])
                last.then_inc(two_filled, 1)

            def weigh(n, g, jj, quarter, first):
                j, half = order[jj], quarter // 2
                if jj == 0 and quarter % 2 == 0 and not first:
                    pe.wait_ge(o_copied, 2 * n - 1 + half)
                if quarter == 0:
                    pe.wait_ge(exp_done, (n * STEPS + jj * GH + GH) * 2)
                lo, hi, edge = quarter * QUARTER, (quarter + 1) * QUARTER, (j + 1) * P
                if not masked_after:
                    pieces = [("all", lo, hi)]
                else:
                    pieces = []
                    if min(hi, edge) > lo:
                        pieces.append(("ones", lo, min(hi, edge)))
                    if hi > max(lo, edge):
                        pieces.append(("all", max(lo, edge), hi))
                    if lo <= j * P < hi:
                        pe.wait_ge(masked, n * NT + jj + 1)
                        pieces.append(("diagonal", j * P, edge))
                for k, (kind, q0, q1) in enumerate(pieces):
                    rows = HD if kind == "diagonal" else HD + 1
                    for hh in range(GH):
                        w = m.w01[:, :] if kind == "ones" else m.vg[:, g, j, hh:hh + GH * (rows - 1) + 1:GH]
                        src = pdiag[:, jj % 2, hh, :] if kind == "diagonal" else probs[:, jj % 4, hh, q0:q1]
                        last = pe.matmul(m.ps_sum[32 * hh:32 * hh + rows, half, q0 - half * CHUNK:q1 - half * CHUNK],
                                         w, src, start=jj == 0 and quarter % 2 == 0 and k == 0,
                                         stop=jj == NT - 1 and k == len(pieces) - 1, skip_group_check=True)
                last.then_inc(pv_done, 1)

            def body(b, g, n_left, first):
                n = b * NG + g
                todo = uses(n_left, first)
                k = 0

                def exponents(jj, hh, half):
                    u = (n * STEPS + jj * GH + hh) * 2 + half
                    if not (first and jj == 0 and hh == 0):
                        pe.wait_ge(exp_done, u - 1)
                    pe.matmul(m.ps_one[:, half, :], m.kx[:, g, hh, order[jj] * P:(order[jj] + 1) * P],
                              m.qx[:, g, hh, half * CHUNK:(half + 1) * CHUNK], start=True, stop=True
                              ).then_inc(t_filled, 1)

                pe.wait_ge(max_loaded, DMA * PARTS * (n + 1))
                for step in range(STEPS):
                    jj, hh = divmod(step, GH)
                    exponents(jj, hh, 0)
                    while k < len(todo) and todo[k][0] == step:
                        _, kind, v = todo[k]
                        count, slot = uses_before(n, n_left, first) + k, (slot_of(g, first) + k) % 2
                        if kind == "score":
                            ahead, sh, i = score_step(v)
                            sg = (g + ahead) % NG
                            if sh == 0 and i == 0:
                                pe.wait_ge(group_loaded[sg], DMA * LOADS * (b + (g + ahead) // NG + 1))
                            slot_free(count)
                            score(sg, sh, i, slot)
                        elif kind == "sums":
                            turn_sums(n - 1, slot, count)
                        else:
                            turn_max((g + 1) % 2, slot, count)
                        k += 1
                    exponents(jj, hh, 1)
                    if jj:
                        weigh(n, g, jj - 1, hh, first)
                    elif not first:
                        weigh(n - 1, (g - 1) % NG, NT - 1, hh, False)

            pe.wait_ge(group_loaded[0], DMA * LOADS)
            for v in range(STEPS):
                slot_free(v, first=v < 2)
                score(0, v // NT, v % NT, v % 2)
            turn_max(0, 0, STEPS)
            over_groups(pe, body)
            for quarter in range(4):
                weigh(n_groups - 1, NG - 1, NT - 1, quarter, False)
            turn_sums(n_groups - 1, uses_in_all % 2, uses_in_all)


def project_out(nc, m):
    with ExitStack() as ctx:
        def sem(name):
            return ctx.enter_context(nc.semaphore(f"o_{name}"))

        s = moment_semaphores(nc, ctx, "o")
        copied = sem("copied")
        turned = sem("turned")
        at_done = sem("at_done")
        mixed = sem("mixed")
        biased = sem("biased")
        added = sem("added")
        mix = ctx.enter_context(nc.sbuf_tensor("mix", [P, 2, CHUNK], F32))
        block = ctx.enter_context(nc.Block())

        @block.scalar
        def _(act):
            def body(t, low, has):
                if has(2):
                    if low + 2 >= 2:
                        act.wait_ge(turned, t + 1)
                    act.activation(m.xn[:, low % 2, :], m.attn[:, chunk_cols(t + 2)], ACT.Copy).then_inc(copied, 1)
                if has(1):
                    h = (low + 1) % 2
                    act.wait_ge(turned, t + 2)
                    act.activation(m.xt[:, h, :], m.ps_one[:, h, :], ACT.Copy).then_inc(at_done, 1)

            over_chunks(act, body, lead=2)

        @block.tensor
        def _(pe):
            def body(t, low, has):
                if has(1):
                    h = (low + 1) % 2
                    pe.wait_ge(copied, t + 2)
                    for k in range(CT):
                        last = pe.transpose(m.ps_one[:, h, k * P:(k + 1) * P], m.xn[:, h, k * P:(k + 1) * P],
                                            m.ident[:, :])
                    last.then_inc(turned, 1)
                if has(0):
                    h = low % 2
                    pe.wait_ge(at_done, t + 1)
                    if low >= 2:
                        pe.wait_ge(biased, t - 1)
                    for k in range(CT):
                        last = pe.matmul(m.ps_two[:, h, k * D:(k + 1) * D], m.xt[:, h, k * P:(k + 1) * P],
                                         m.w_out[:, :], start=True, stop=True, skip_group_check=True)
                    last.then_inc(mixed, 1)

            over_chunks(pe, body, lead=1, start=2)

        @block.gpsimd
        def _(pool):
            def body(t, low, has):
                x = m.x[:, chunk_cols(t)]
                hold(pool, biased, t + 1, m.passed_pool)
                pool.tensor_tensor(x, x, mix[:, low % 2, :], ALU.add).then_inc(added, 1)
                if low > 0:
                    deviations(pool, m, s, t - 1, 1 - low % 2)

            pool.sem_inc(s.rstd_done, 2)
            over_chunks(pool, body, start=2)
            deviations(pool, m, s, CHUNKS - 1, 1)

        @block.vector
        def _(dve):
            def body(t, low, has):
                if has(2):
                    h = low % 2
                    dve.wait_ge(mixed, t + 3)
                    if low >= 0:
                        dve.wait_ge(added, t + 1)
                    bias = m.b_out[:, :].unsqueeze(1).to_broadcast([P, CT, D])
                    dve.tensor_tensor(mix[:, h, :].rearrange("p (t d) -> p t d", t=CT),
                                      m.ps_two[:, h, 0:CHUNK].rearrange("p (t d) -> p t d", t=CT),
                                      bias, ALU.add).then_inc(biased, 1)
                if has(0):
                    hold(dve, added, t + 1, m.passed_dve)
                    moments(dve, m, s, t, low % 2)

            over_chunks(dve, body, lead=2)


class ExpertOperands:

    def __init__(self, nc, ctx, layer):
        def sb(name, shape):
            return ctx.enter_context(nc.sbuf_tensor(f"{layer}_{name}", shape, F32R))

        self.x_hi, self.x_lo = (sb(name, [P, B * S]) for name in ("x_hi", "x_lo"))
        self.w_hi, self.w_lo = (sb(name, [P, 2, NE, D]) for name in ("w_hi", "w_lo"))


def route(nc, m, ops, layer):
    with ExitStack() as ctx:
        def sem(name):
            return ctx.enter_context(nc.semaphore(f"{layer}r_{name}"))

        s = norm_semaphores(nc, ctx, f"{layer}r")
        kept = sem("kept")
        x_split = sem("x_split")
        w_high = sem("w_high")
        scored, taken = sem("scored"), sem("taken")
        step, exped, ranked = sem("step"), sem("exped"), sem("ranked")
        room = ctx.enter_context(nc.sbuf_tensor(f"{layer}r_room", [P, (8 * E + 4) * TILES], F32))

        def scratch(n):
            return room[:, n * TILES * E:(n + 1) * TILES * E].rearrange("p (t e) -> p t e", e=E)

        logits, prob, sel, eq, rank, hot, sel2, hot2 = (scratch(n) for n in range(8))
        small = room[:, 8 * TILES * E:].rearrange("p (k t) -> p k t", k=4)
        block = ctx.enter_context(nc.Block())

        @block.gpsimd
        def _(pool):
            for e in range(E):
                pool.memset(rank[:, :, e:e + 1], float(E - e)).then_inc(ranked, 1)
            for n, w in enumerate((m.w1, m.w3)):
                pool.tensor_scalar(ops.w_hi[:, n, :, :], w[:, :, :], 1.0, 0.0, ALU.mult, ALU.add).then_inc(w_high, 1)
                pool.wait_ge(w_high, n + 1)
                pool.tensor_tensor(ops.w_lo[:, n, :, :], w[:, :, :], ops.w_hi[:, n, :, :].bitcast(F32), ALU.subtract)

        @block.scalar
        def _(act):
            def body(t, low, has):
                h = low % 2
                act.wait_ge(s.turned, t + 1)
                if low >= 2:
                    act.wait_ge(scored, t - 1)
                act.activation(m.xt[:, h, :], m.ps_one[:, h, :], ACT.Copy).then_inc(s.xt_done, 1)
                act.activation(ops.x_hi[:, chunk_cols(t)], m.ps_one[:, h, :], ACT.Copy).then_inc(kept, 1)

            over_chunks(act, body, start=2)
            act.wait_ge(step, 2)
            act.activation(prob, prob, ACT.Exp).then_inc(exped, 1)

        @block.tensor
        def _(pe):
            def body(t, low, has):
                if has(1):
                    if low + 1 >= 2:
                        pe.wait_ge(x_split, t)
                    norm_pe_turn(pe, m, s, t + 1, low + 1)
                if has(0):
                    h = low % 2
                    pe.wait_ge(s.xt_done, t + 1)
                    if low >= 2:
                        pe.wait_ge(taken, t - 1)
                    for k in range(CT):
                        last = pe.matmul(m.ps_sum[:, h, k * E:(k + 1) * E], m.xt[:, h, k * P:(k + 1) * P],
                                         m.w_router[:, :], start=True, stop=True, skip_group_check=True)
                    last.then_inc(scored, 1)

            over_chunks(pe, body, lead=1, start=2)

        @block.vector
        def _(dve):
            flat = room[:, 0:TILES * E]
            def body(t, low, has):
                if has(2):
                    norm_dve_apply(dve, m, s, t + 2, low + 2)
                if has(0):
                    dve.wait_ge(kept, t + 1)
                    dve.tensor_tensor(ops.x_lo[:, chunk_cols(t)], m.ps_one[:, low % 2, :],
                                      ops.x_hi[:, chunk_cols(t)].bitcast(F32), ALU.subtract).then_inc(x_split, 1)
                    dve.wait_ge(scored, t + 1)
                    dve.tensor_copy(flat[:, bass.ds(t * (CT * E), CT * E)], m.ps_sum[:, low % 2, 0:CT * E]
                                    ).then_inc(taken, 1)

            over_chunks(dve, body, lead=2)

            def wide(k):
                return small[:, k, :].unsqueeze(2).to_broadcast([P, TILES, E])

            done = [0]

            def chain(ins):
                done[0] += 1
                ins.then_inc(step, 1)
                dve.wait_ge(step, done[0])

            dve.wait_ge(taken, CHUNKS)
            chain(dve.tensor_reduce(small[:, 0, :], logits, AX.X, ALU.max))
            chain(dve.tensor_tensor(prob, logits, wide(0), ALU.subtract))
            dve.wait_ge(exped, 1)
            chain(dve.tensor_reduce(small[:, 1, :], prob, AX.X, ALU.add))
            chain(dve.reciprocal(small[:, 1, :], small[:, 1, :]))
            chain(dve.tensor_tensor(prob, prob, wide(1), ALU.mult))
            bias = m.e_bias[:, :].unsqueeze(1).to_broadcast([P, TILES, E])
            chain(dve.tensor_tensor(sel, prob, bias, ALU.add))
            dve.wait_ge(ranked, E)
            for src, out in ((sel, hot), (sel2, hot2)):
                chain(dve.tensor_reduce(small[:, 2, :], src, AX.X, ALU.max))
                chain(dve.tensor_tensor(eq, src, wide(2), ALU.is_equal))
                chain(dve.tensor_tensor(eq, eq, rank, ALU.mult))
                chain(dve.tensor_reduce(small[:, 3, :], eq, AX.X, ALU.max))
                chain(dve.tensor_tensor(out, rank, wide(3), ALU.is_equal))
                if out is hot:
                    chain(dve.scalar_tensor_tensor(sel2, hot, -3.0e38, sel, ALU.mult, ALU.add))
            chain(dve.tensor_tensor(hot, hot, hot2, ALU.add))
            chain(dve.tensor_tensor(m.gates[:, :, 0:E], hot, prob, ALU.mult))


def experts(nc, m, ops, layer, out, loads):
    last_layer = out is not None
    UNITS = HALVES * NE
    with ExitStack() as ctx:
        def sem(name):
            return ctx.enter_context(nc.semaphore(f"{layer}e_{name}"))

        def sb(name, shape, dt=F32):
            return ctx.enter_context(nc.sbuf_tensor(f"{layer}e_{name}", shape, dt))

        h_done = sem("h_done")
        s_done = sem("s_done")
        a_done = sem("a_done")
        y_done = sem("y_done")
        acc_done = sem("acc_done")
        begun = sem("begun")
        if last_layer:
            stored = [sem(f"stored{h}") for h in range(2)]
            acc_free = sem("acc_free")
        else:
            loaded = sem("loaded")
            put = sem("put")
            s = moment_semaphores(nc, ctx, f"{layer}e")
        silu, hid = m.xn, m.xt
        acc = sb("acc", [P, 2, CHUNK])
        gate = sb("gate", [P, 2, CT, NE])
        gates_flat = m.gates[:, :, :].rearrange("p t e -> p (t e)")
        block = ctx.enter_context(nc.Block())

        @block.tensor
        def _(pe):
            def hidden(b, k):
                h, e = divmod(k, NE)
                x_hi, x_lo = (x[:, bass.ds((b * 2 + h) * CHUNK, CHUNK)] for x in (ops.x_hi, ops.x_lo))
                for w in range(2):
                    for i, (weights, x) in enumerate(((ops.w_hi, x_hi), (ops.w_hi, x_lo), (ops.w_lo, x_hi))):
                        last = pe.matmul(m.ps_two[:, k % 2, w * CHUNK:(w + 1) * CHUNK], weights[:, w, e, :], x, start=i == 0, stop=i == 2)
                last.then_inc(h_done, 1)

            def output(b, k):
                e, unit = k % NE, b * UNITS + k
                pe.wait_ge(a_done, unit + 1)
                if k >= 2:
                    pe.wait_ge(acc_done, (unit - 1) * CT)
                for t in range(CT):
                    last = pe.matmul(m.ps_one[:, k % 2, t * D:(t + 1) * D], hid[:, k % 2, t * P:(t + 1) * P],
                                     m.w2[:, e, :], start=True, stop=True, skip_group_check=True)
                last.then_inc(y_done, 1)

            with pe.Fori(0, B) as b:
                hidden(b, 0)
                for k in range(UNITS):
                    if k + 1 < UNITS:
                        hidden(b, k + 1)
                    output(b, k)
                pe.wait_ge(acc_done, (b + 1) * (UNITS * CT))

        @block.scalar
        def _(act):
            with act.Fori(0, B) as b:
                for k in range(UNITS):
                    act.wait_ge(h_done, b * UNITS + k + 1)
                    act.activation(silu[:, k % 2, :], m.ps_two[:, k % 2, 0:CHUNK], ACT.Silu).then_inc(s_done, 1)

        if not last_layer:
            @block.gpsimd
            def _(pool):
                pool.sem_inc(s.rstd_done, 2)
                over_chunks(pool, lambda t, low, has: deviations(pool, m, s, t, low % 2))

        @block.vector
        def _(dve):
            def begin(b, h):
                chunk = b * 2 + h
                if last_layer:
                    dve.wait_ge(acc_free, chunk + 1)
                dve.tensor_copy(acc[:, h, :], m.x[:, chunk_cols(chunk)]).then_inc(begun, 1)
                dve.tensor_copy(gate[:, h, :, :].rearrange("p t e -> p (t e)"),
                                gates_flat[:, bass.ds(chunk * (CT * NE), CT * NE)]).then_inc(begun, 1)

            def gather(b, k):
                h, e = divmod(k, NE)
                before = (b * UNITS + k) * CT
                dve.wait_ge(y_done, b * UNITS + k + 1)
                if e == 0:
                    dve.wait_ge(begun, (b * 2 + h) * 2 + 2)
                else:
                    dve.wait_ge(acc_done, before)
                for t in range(CT):
                    part = acc[:, h, t * D:(t + 1) * D]
                    dve.scalar_tensor_tensor(part, m.ps_one[:, k % 2, t * D:(t + 1) * D], gate[:, h, t, e:e + 1],
                                             part, ALU.mult, ALU.add).then_inc(acc_done, 1)
                if e == NE - 1:
                    hold(dve, acc_done, before + CT, m.passed_dve)
                    if not last_layer:
                        dve.tensor_copy(m.x[:, chunk_cols(b * 2 + h)], acc[:, h, :]).then_inc(put, 1)
                        dve.wait_ge(put, b * 2 + h + 1)
                        moments(dve, m, s, b * 2 + h, h)

            with dve.Fori(0, B) as b:
                for k in range(UNITS):
                    if k % NE == 0:
                        begin(b, k // NE)
                    dve.wait_ge(s_done, b * UNITS + k + 1)
                    dve.tensor_tensor(hid[:, k % 2, :], silu[:, k % 2, :], m.ps_two[:, k % 2, CHUNK:2 * CHUNK],
                                      ALU.mult).then_inc(a_done, 1)
                    if k:
                        gather(b, k - 1)
                gather(b, UNITS - 1)

        @block.sync
        def _(sp):
            if last_layer:
                sp.sem_inc(acc_free, 2)
                rows = out.rearrange("b (h t p) d -> p b h t d", p=P, t=CT)
                with sp.Fori(0, B) as b:
                    for h in range(2):
                        sp.wait_ge(acc_done, (b * UNITS + (h + 1) * NE) * CT)
                        sp.dma_start(rows[:, bass.ds(b, 1), h, :, :].rearrange("p b t d -> p (b t) d"),
                                     acc[:, h, :].rearrange("p (t d) -> p t d", t=CT)).then_inc(stored[h], DMA)
                        sp.wait_ge(stored[h], DMA * (b + 1))
                        sp.sem_inc(acc_free, 1)
            else:
                for dst, src in loads:
                    sp.dma_start(dst, src).then_inc(loaded, DMA)
                sp.wait_ge(loaded, DMA * len(loads))


def build(nc, a, out):
    with ExitStack() as ctx:
        m = allocate(nc, ctx)
        group_loaded = {layer: [ctx.enter_context(nc.semaphore(f"{layer}_group_loaded{g}")) for g in range(NG)]
                        for layer in "ab"}
        expert_loads = [
            (m.w_out[:, :], a["b_wout"]), (m.b_out[:, :], a["b_bias"].partition_broadcast(P)),
            (m.w_router[:, :], a["router"]), (m.e_bias[:, :], a["e_bias"].partition_broadcast(P)),
        ]
        for w, routed, shared in ((m.w1, "w1", "sw1"), (m.w3, "w3", "sw3"), (m.w2, "w2", "sw2")):
            expert_loads += [(w[:, 0:E, :], a[routed].rearrange("e i o -> i e o")), (w[:, E, :], a[shared])]
        setup(nc, m, a)
        project(nc, m, "a", expert_loads, group_loaded["a"])
        attend(nc, m, "a", group_loaded["a"])
        with ExitStack() as ffn:
            ops = ExpertOperands(nc, ffn, "a")
            route(nc, m, ops, "a")
            experts(nc, m, ops, "a", None, [
                (m.w_q[:, 0, 0, :], a["b_wq"]), (m.w_q[:, 1, 0, :], a["b_wk"]),
                (m.w_q[:, 0, 1, :], a["b_wq_swapped"]), (m.w_q[:, 1, 1, :], a["b_wk_swapped"]),
                (m.w_v[:, :], a["b_wv"]), (m.rope, a["rope"]),
            ])
        project(nc, m, "b", [], group_loaded["b"])
        attend(nc, m, "b", group_loaded["b"])
        project_out(nc, m)
        with ExitStack() as ffn:
            ops = ExpertOperands(nc, ffn, "b")
            route(nc, m, ops, "b")
            experts(nc, m, ops, "b", out, [])




def _layout(i):
    perm = np.arange(D).reshape(NG, GH, HD).transpose(0, 2, 1).reshape(-1)
    swap = np.roll(np.arange(D).reshape(NG, GH, HD), HD // 2, axis=2).transpose(0, 2, 1).reshape(-1)
    qkv = np.asarray(i["L0_attn_b_w_qkv"]).T
    wq, wk, wv = qkv[:, 0:D], qkv[:, D:2 * D], qkv[:, 2 * D:3 * D]
    return {
        "x": i["L0_attn_a_content"],
        "a_wq": i["L0_attn_a_Wq"][:, perm], "a_wk": i["L0_attn_a_Wk"][:, perm], "a_wv": i["L0_attn_a_Wv"][:, perm],
        "b_wq": wq[:, perm], "b_wk": wk[:, perm], "b_wv": wv[:, perm],
        "b_wq_swapped": wq[:, swap], "b_wk_swapped": wk[:, swap],
        "b_wout": np.asarray(i["L0_attn_b_w_out"]).T, "b_bias": i["L0_attn_b_b_out"],
        "router": i["L0_ffn_router_w"], "e_bias": i["L0_ffn_expert_bias"],
        "w1": i["L0_ffn_w1"], "w2": i["L0_ffn_w2"], "w3": i["L0_ffn_w3"],
        "sw1": i["L0_ffn_sw1"], "sw2": i["L0_ffn_sw2"], "sw3": i["L0_ffn_sw3"],
    }


def _rope_tables():
    half = HD // 2
    inv = (1.0 / 10000.0 ** (np.arange(0, HD, 2, dtype=np.float32) / np.float32(HD))).astype(np.float32)
    angle = (np.arange(S, dtype=np.float32)[:, None] * inv[None, :]).astype(np.float32).astype(np.float64)
    cos, sin = np.cos(angle).T, np.sin(angle).T
    rows = np.stack([np.concatenate([cos, cos]), np.concatenate([-sin, sin])])
    rows = np.broadcast_to(rows[:, None, :, None, :], (2, NG, 2 * half, GH, S)).reshape(2, P, S)
    return np.ascontiguousarray(rows.transpose(1, 0, 2)).astype(np.float32)


def kernel(**inputs):
    import concourse.bacc as bacc
    from concourse.bass_utils import run_bass_kernel_spmd

    nc = bacc.Bacc("TRN2", target_bir_lowering=False, num_devices=1)
    arrays = {f"in_{k}": np.ascontiguousarray(v) for k, v in _layout({k: np.asarray(v) for k, v in inputs.items()}).items()}
    arrays["in_rope"] = _rope_tables()
    args = {k[3:]: nc.dram_tensor(k, v.shape, F32, kind="ExternalInput").ap() for k, v in arrays.items()}
    out = nc.dram_tensor("out_dram", (B, S, D), F32, kind="ExternalOutput").ap()
    build(nc, args, out)
    r = run_bass_kernel_spmd(nc, [arrays], core_ids=[0])
    return r.results[0]["out_dram"]
```

```python
from contextlib import ExitStack

import numpy as np

import concourse.bass as bass
from concourse import mybir

F32 = mybir.dt.float32
BF16 = mybir.dt.bfloat16
F32R = mybir.dt.float32r
ALU = mybir.AluOpType
ACT = mybir.ActivationFunctionType
AX = mybir.AxisListType

P = 128
B = 4
S = 1024
D = 128
HD = 8
NG = 4
GH = 4
GR = GH * HD
NT = S // P
TILES = B * NT
CHUNK = 512
CT = CHUNK // P
CHUNKS = B * S // CHUNK
HALVES = S // CHUNK
E = 8
NE = E + 1
PARTS = 3
PR = 32
MAXROW = PARTS * PR
VW = (HD + 1) * GH
EPS = 1e-5
SCALE = float(HD) ** -0.5
DMA = 16


class Buffers:
    pass


def allocate(nc, ctx):
    m = Buffers()

    def sb(name, shape, dt=F32):
        return ctx.enter_context(nc.sbuf_tensor(name, shape, dt))

    m.x = sb("x", [P, TILES * D])
    m.attn = sb("attn", [P, TILES * D])
    m.ident = sb("ident", [P, P])
    m.w_q = sb("w_q", [P, 2, 2, D])
    m.w_v = sb("w_v", [P, D])
    m.w_out = sb("w_out", [P, D])
    m.b_out = sb("b_out", [P, D])
    m.rope = m.attn[:, 0:2 * S].rearrange("p (k s) -> p k s", k=2)
    m.w_router = sb("w_router", [P, E])
    m.e_bias = sb("e_bias", [P, E])
    m.w1 = sb("w1", [P, NE, D])
    m.w2 = sb("w2", [P, NE, D])
    m.w3 = sb("w3", [P, NE, D])
    m.gates = sb("gates", [P, TILES, NE])
    m.xn = sb("xn", [P, 2, CHUNK])
    m.xt = sb("xt", [P, 2, CHUNK])
    m.stats = sb("stats", [P, 2, CT, 6])
    m.mv = sb("mv", [P, 2, CT, 2])
    m.shifted = sb("shifted", [P, 2, CT])
    m.mean = sb("mean", [P, TILES])
    m.rstd = sb("rstd", [P, TILES])
    m.expo = sb("expo", [P, CT])
    m.qx = sb("qx", [P, NG, GH, S], BF16)
    m.kx = sb("kx", [P, NG, GH, S], BF16)
    m.vg = sb("vg", [P, NG, NT, VW])
    m.causal = sb("causal", [P, P])
    m.w01 = sb("w01", [P, HD + 1])
    m.ps_one = ctx.enter_context(nc.psum_tensor("ps_one", [P, 2, CHUNK], F32))
    m.ps_two = ctx.enter_context(nc.psum_tensor("ps_two", [P, 2, 2 * CHUNK], F32))
    m.ps_sum = ctx.enter_context(nc.psum_tensor("ps_sum", [P, 2, CHUNK], F32))
    m.qk_parts = nc.dram_tensor("qk_parts", (B, PARTS, 2, P, S), BF16, kind="Internal").ap()
    m.v_rows = nc.dram_tensor("v_rows", (B, NT, P, D), F32, kind="Internal").ap()
    m.passed_dve, m.passed_pool = (ctx.enter_context(nc.semaphore(name)) for name in ("passed_dve", "passed_pool"))
    return m


def tile_cols(tile):
    return bass.ds(tile * D, D)


def chunk_cols(chunk):
    return bass.ds(chunk * CHUNK, CHUNK)


def hold(eng, sem, value, passed):
    eng.wait_ge(sem, value)
    eng.sem_inc(passed, 1)


def over_chunks(eng, body, lead=0, start=0):
    pairs = (CHUNKS - lead - start) // 2

    def run(t, low, high):
        body(t, low, lambda k: low + k >= 0 and high + k < CHUNKS)

    for t in range(-lead, start):
        run(t, t, t)
    with eng.Fori(0, pairs) as i:
        for h in range(2):
            run(i * 2 + (start + h), start + h, start + h + 2 * pairs - 2)
    for t in range(start + 2 * pairs, CHUNKS):
        run(t, t, t)


def moment_semaphores(nc, ctx, tag):
    def sem(name):
        return ctx.enter_context(nc.semaphore(f"{tag}_{name}"))

    s = Buffers()
    s.moments = sem("moments")
    s.stats_done = sem("stats_done")
    s.stats_kept = sem("stats_kept")
    s.shifted = sem("shifted")
    s.rstd_done = sem("rstd_done")
    return s


def moments(dve, m, s, chunk, h):
    tile_sums(dve, m, s, chunk, h)
    tile_moments(dve, m, s, chunk, h)


def tile_sums(dve, m, s, chunk, h):
    hold(dve, s.rstd_done, chunk + 1, m.passed_dve)
    for t in range(CT):
        dve.bn_stats(m.stats[:, h, t, :], m.x[:, tile_cols(chunk * CT + t)]).then_inc(s.moments, 1)


def tile_moments(dve, m, s, chunk, h):
    hold(dve, s.moments, chunk * CT + CT, m.passed_dve)
    for t in range(CT):
        dve.bn_aggr(m.mv[:, h, t, :], m.stats[:, h, t, :]).then_inc(s.stats_done, 1)
    hold(dve, s.stats_done, chunk * CT + CT, m.passed_dve)
    dve.tensor_copy(m.mean[:, bass.ds(chunk * CT, CT)], m.mv[:, h, :, 0]).then_inc(s.stats_kept, 1)


def deviations(pool, m, s, chunk, h):
    hold(pool, s.stats_kept, chunk + 1, m.passed_pool)
    pool.tensor_scalar(m.shifted[:, h, :], m.mv[:, h, :, 1], EPS, 0.0, ALU.add, ALU.add).then_inc(s.shifted, 1)
    hold(pool, s.shifted, chunk + 1, m.passed_pool)
    pool.tensor_tensor(m.rstd[:, bass.ds(chunk * CT, CT)], m.shifted[:, h, :], m.expo[:, :],
                       ALU.pow).then_inc(s.rstd_done, 1)


def setup(nc, m, a):
    with ExitStack() as ctx:
        x_loaded = [ctx.enter_context(nc.semaphore(f"x_loaded{b}")) for b in range(B)]
        loaded = ctx.enter_context(nc.semaphore("loaded"))
        cleared = ctx.enter_context(nc.semaphore("cleared"))
        s = moment_semaphores(nc, ctx, "s")
        block = ctx.enter_context(nc.Block())
        loads = [
            (m.w_q[:, 0, 0, :], a["a_wq"]),
            (m.w_q[:, 1, 0, :], a["a_wk"]),
            (m.w_v[:, :], a["a_wv"]),
        ]

        @block.sync
        def _(sp):
            for b in range(B):
                sp.dma_start(m.x[:, b * NT * D:(b + 1) * NT * D].rearrange("p (t d) -> p t d", d=D),
                             a["x"][b, :, :].rearrange("(t p) d -> p t d", p=P)).then_inc(x_loaded[b], DMA)
            for out, src in loads:
                sp.dma_start(out, src).then_inc(loaded, DMA)
            sp.wait_ge(loaded, DMA * len(loads))

        @block.gpsimd
        def _(pool):
            pool.memset(m.kx[:, :, :, :].bitcast(F32), 0.0).then_inc(cleared, 1)
            pool.memset(m.ident[:, :], 0.0).then_inc(cleared, 1)
            pool.memset(m.w01[:, :], 0.0).then_inc(cleared, 1)
            pool.memset(m.causal[:, :], 1.0).then_inc(cleared, 1)
            pool.memset(m.expo[:, :], -0.5)
            pool.memset(m.vg[:, :, :, GR:VW], 1.0)
            pool.memset(m.gates[:, :, E:NE], 1.0)
            pool.wait_ge(cleared, 4)
            pool.affine_select(out=m.causal[:, :], in_=m.causal[:, :], compare_op=ALU.is_ge, fill=0.0,
                               base=0, pattern=[[1, P]], channel_multiplier=-1)
            pool.affine_select(out=m.ident[:, :], in_=m.ident[:, :], compare_op=ALU.not_equal, fill=1.0,
                               base=0, pattern=[[-1, P]], channel_multiplier=1)
            pool.memset(m.w01[:, HD:HD + 1], 1.0)
            pool.sem_inc(s.rstd_done, 2)
            for chunk in range(CHUNKS):
                deviations(pool, m, s, chunk, chunk % 2)

        @block.vector
        def _(dve):
            for chunk in range(CHUNKS):
                dve.wait_ge(x_loaded[chunk // HALVES], DMA)
                moments(dve, m, s, chunk, chunk % 2)


def norm_semaphores(nc, ctx, tag):
    def sem(name):
        return ctx.enter_context(nc.semaphore(f"{tag}_{name}"))

    s = Buffers()
    s.xn_done = sem("xn_done")
    s.turned = sem("turned")
    s.xt_done = sem("xt_done")
    return s


def norm_dve_apply(dve, m, s, chunk, low):
    if low >= 2:
        dve.wait_ge(s.turned, chunk - 1)
    for t in range(CT):
        tile = chunk * CT + t
        dve.tensor_scalar(m.xn[:, low % 2, t * P:(t + 1) * P], m.x[:, tile_cols(tile)],
                          m.mean[:, bass.ds(tile, 1)], m.rstd[:, bass.ds(tile, 1)],
                          ALU.subtract, ALU.mult).then_inc(s.xn_done, 1)


def norm_pe_turn(pe, m, s, chunk, low):
    h = low % 2
    pe.wait_ge(s.xn_done, chunk * CT + CT)
    if low >= 2:
        pe.wait_ge(s.xt_done, chunk - 1)
    for t in range(CT):
        last = pe.transpose(m.ps_one[:, h, t * P:(t + 1) * P], m.xn[:, h, t * P:(t + 1) * P], m.ident[:, :])
    last.then_inc(s.turned, 1)


LOADS = 2 * PARTS + 1


def load_group(sp, m, b, g, group_loaded):
    for p in range(PARTS):
        rows = slice(p * PR, p * PR + PARTS * HD)
        for c, (dst, first_part, parts) in enumerate(((m.qx, p, 1), (m.kx, 0, PARTS))):
            src = m.qk_parts[bass.ds(b, 1), first_part:first_part + parts, c, g * GR:(g + 1) * GR, :]
            src = src.rearrange("b c (d h) s -> (b c) d (h s)", h=GH)
            sp.dma_start(dst[rows, g, :, :].rearrange("p h s -> p (h s)"),
                         src.to_broadcast([PARTS, HD, GH * S])).then_inc(group_loaded[g], DMA)
    sp.dma_start(m.vg[:, g, :, 0:GR],
                 m.v_rows[bass.ds(b, 1), :, :, g * GR:(g + 1) * GR].rearrange("b t p r -> p (b t) r")
                 ).then_inc(group_loaded[g], DMA)


STEPS = NT * GH


class Scores:

    def __init__(self, nc, ctx, layer):
        self.filled = ctx.enter_context(nc.semaphore(f"{layer}_two_filled"))
        self.read = ctx.enter_context(nc.semaphore(f"{layer}_two_read"))
        self.negmax = ctx.enter_context(nc.sbuf_tensor(f"{layer}_negmax", [P, 2, STEPS], F32))


def score(pe, m, sc, g, hh, i, slot):
    for half in range(2):
        last = pe.matmul(m.ps_two[:, slot, half * CHUNK:(half + 1) * CHUNK],
                         m.qx[0:MAXROW, g, hh, i * P:(i + 1) * P],
                         m.kx[0:MAXROW, g, hh, half * CHUNK:(half + 1) * CHUNK], start=True, stop=True)
    last.then_inc(sc.filled, 1)


def take_max(dve, m, sc, parity, hh, i, slot, count):
    dve.wait_ge(sc.filled, count + 1)
    dve.tensor_reduce(sc.negmax[:, parity, hh * NT + i:hh * NT + i + 1], m.ps_two[:, slot, :],
                      AX.X, ALU.max, negate=True).then_inc(sc.read, 1)


def project(nc, m, layer, later, group_loaded, sc):
    rope = layer == "b"
    with ExitStack() as ctx:
        def sem(name):
            return ctx.enter_context(nc.semaphore(f"{layer}p_{name}"))

        def sb(name, shape, dt=F32):
            return ctx.enter_context(nc.sbuf_tensor(f"{layer}p_{name}", shape, dt))

        s = norm_semaphores(nc, ctx, f"{layer}p")
        later_loaded = sem("later_loaded")
        qk_done = sem("qk_done")
        v_done = sem("v_done")
        v_copied = sem("v_copied")
        product = sem("product")
        rotated = sem("rotated")
        high = sem("high")
        rest1 = sem("rest1")
        middle = sem("middle")
        low_done = sem("low_done")
        zeroed = sem("zeroed")
        ones_set = sem("ones_set")
        first_stored = sem("first_stored")
        others_stored = sem("others_stored")
        v_stored = [sem(f"v_stored{h}") for h in range(2)]
        v_free = sem("v_free")
        pbuf = sb("parts", [P, CHUNKS * PARTS, 2 * CHUNK], BF16)
        vbuf = sb("vbuf", [P, 2, CHUNK])
        rest = sb("rest", [P, 2, 2 * CHUNK])
        prod_c = sb("prod_c", [P, 2, 2 * CHUNK])
        prod_s = sb("prod_s", [P, 2 * CHUNK])[:, :]
        USES = 2 if rope else 1

        def source(h):
            return prod_c[:, h, :] if rope else m.ps_two[:, h, :]

        def part(chunk, c):
            return pbuf[:, bass.ds(chunk * PARTS + c, 1), :].rearrange("p u n -> p (u n)")

        block = ctx.enter_context(nc.Block())

        @block.sync
        def _(sp):
            for out, src in later:
                sp.dma_start(out, src).then_inc(later_loaded, DMA)
            sp.sem_inc(v_free, 2)

            def store(b, h, parts_stored):
                chunk = b * 2 + h
                sp.wait_ge(v_copied, chunk + 1)
                tokens = m.v_rows[bass.ds(b, 1), h * CT:(h + 1) * CT, :, :].rearrange("b t p r -> p (b t) r")
                sp.dma_start(tokens, vbuf[:, h, :].rearrange("p (t r) -> p t r", t=CT)).then_inc(v_stored[h], DMA)
                for c, part_done in enumerate((high, middle, low_done)):
                    if c == PARTS - 1:
                        sp.wait_ge(v_stored[h], (b + 1) * DMA)
                        sp.sem_inc(v_free, 1)
                    sp.wait_ge(part_done, chunk + 1)
                    rows = m.qk_parts[bass.ds(b, 1), c, :, :, h * CHUNK:(h + 1) * CHUNK]
                    sp.dma_start(rows.rearrange("b i p n -> p (b i) n"),
                                 part(chunk, c).rearrange("p (i n) -> p i n", i=2)).then_inc(parts_stored, DMA)

            for h in range(2):
                store(0, h, first_stored)
            for h in range(2):
                store(1, h, others_stored)
            if not rope:
                sp.wait_ge(zeroed, NG)
            sp.wait_ge(first_stored, DMA * PARTS * HALVES)
            load_group(sp, m, 0, 0, group_loaded)
            with sp.Fori(0, B - 2) as b:
                for h in range(2):
                    store(b + 2, h, others_stored)
            for g in range(1, 3):
                load_group(sp, m, 0, g, group_loaded)
            sp.wait_ge(others_stored, DMA * PARTS * (CHUNKS - HALVES))
            if later:
                sp.wait_ge(later_loaded, DMA * len(later))

        @block.gpsimd
        def _(pool):
            if not rope:
                pool.memset(m.kx[MAXROW:MAXROW + PARTS, :, :, :], 1.0).then_inc(ones_set, 1)
                pool.wait_ge(ones_set, 1)

            def body(t, low, has):
                if rope and has(2):
                    chunk, h = t + 2, low % 2
                    pool.wait_ge(product, chunk * 2 + 2)
                    pool.tensor_tensor(prod_c[:, h, :], prod_c[:, h, :], prod_s, ALU.add
                                       ).then_inc(rotated, 1)
                if has(0):
                    h = low % 2
                    hold(pool, middle, t + 1, m.passed_pool)
                    pool.tensor_tensor(part(t, 2), rest[:, h, :], part(t, 1), ALU.subtract
                                       ).then_inc(low_done, 1)

            over_chunks(pool, body, lead=2)

        @block.vector
        def _(dve):
            def body(t, low, has):
                if has(3):
                    norm_dve_apply(dve, m, s, t + 3, low + 3)
                if not rope and low == -1:
                    for g in range(NG):
                        dve.memset(m.qx[:, g, :, :].bitcast(F32), 0.0).then_inc(zeroed, 1)
                if rope and has(1):
                    chunk, h = t + 1, (low + 1) % 2
                    if low + 1 >= 2:
                        dve.wait_ge(rest1, chunk - 1)
                    for n in range(2):
                        if n and low + 1 >= 1:
                            dve.wait_ge(rotated, chunk)
                        dve.wait_ge(qk_done, chunk * 2 + n + 1)
                        half = low + 1 & 1
                        table = m.rope[:, n, half * CHUNK:(half + 1) * CHUNK].unsqueeze(1).to_broadcast([P, 2, CHUNK])
                        dve.tensor_tensor((prod_s if n else prod_c[:, h, :]).rearrange("p (i n) -> p i n", i=2),
                                          m.ps_two[:, n, :].rearrange("p (i n) -> p i n", i=2), table,
                                          ALU.mult).then_inc(product, 1)
                if has(0):
                    h = low % 2
                    dve.wait_ge(high, t + 1)
                    if low >= 2:
                        dve.wait_ge(low_done, t - 1)
                    dve.tensor_tensor(rest[:, h, :], source(h), part(t, 0), ALU.subtract).then_inc(rest1, 1)

            over_chunks(dve, body, lead=3, start=2)
            for v in range(STEPS):
                take_max(dve, m, sc, 0, v // NT, v % NT, v % 2, v)

        @block.scalar
        def _(act):
            def body(t, low, has):
                if has(3):
                    h = (low + 3) % 2
                    act.wait_ge(s.turned, t + 4)
                    act.activation(m.xt[:, h, :], m.ps_one[:, h, :], ACT.Copy).then_inc(s.xt_done, 1)
                if has(1):
                    chunk, h = t + 1, (low + 1) % 2
                    if rope:
                        act.wait_ge(rotated, chunk + 1)
                    else:
                        act.wait_ge(qk_done, chunk + 1)
                    act.activation(part(chunk, 0), source(h), ACT.Copy).then_inc(high, 1)
                if has(0):
                    h = low % 2
                    act.wait_ge(rest1, t + 1)
                    act.activation(part(t, 1), rest[:, h, :], ACT.Copy).then_inc(middle, 1)
                if has(1):
                    chunk, h = t + 1, (low + 1) % 2
                    act.wait_ge(v_free, chunk + 1)
                    act.wait_ge(v_done, chunk + 1)
                    act.activation(vbuf[:, h, :], m.ps_sum[:, h, :], ACT.Copy).then_inc(v_copied, 1)

            over_chunks(act, body, lead=3)

        @block.tensor
        def _(pe):
            def body(t, low, has):
                if has(1):
                    norm_pe_turn(pe, m, s, t + 1, low + 1)
                if has(0):
                    h = low % 2
                    pe.wait_ge(s.xt_done, t + 1)
                    for n in range(USES):
                        slot = n if rope else h
                        if rope and low >= 1:
                            pe.wait_ge(product, t * 2 + n - 1)
                        if not rope and low >= 2:
                            pe.wait_ge(rest1, t - 1)
                        for i in range(2):
                            last = pe.matmul(m.ps_two[:, slot, i * CHUNK:(i + 1) * CHUNK],
                                             m.w_q[:, i, n, :], m.xt[:, h, :], start=True, stop=True)
                        last.then_inc(qk_done, 1)
                    if low >= 2:
                        pe.wait_ge(v_copied, t - 1)
                    for k in range(CT):
                        last = pe.matmul(m.ps_sum[:, h, k * D:(k + 1) * D], m.xt[:, h, k * P:(k + 1) * P],
                                         m.w_v[:, :], start=True, stop=True, skip_group_check=True)
                    last.then_inc(v_done, 1)

            over_chunks(pe, body, lead=1, start=2)
            pe.wait_ge(group_loaded[0], DMA * LOADS)
            for v in range(STEPS):
                if v == 0:
                    pe.wait_ge(product if rope else rest1, 2 * CHUNKS if rope else CHUNKS)
                if v >= 2:
                    pe.wait_ge(sc.read, v - 1)
                score(pe, m, sc, 0, v // NT, v % NT, v % 2)


def attend(nc, m, layer, group_loaded, sc):
    masked_after = layer == "a"
    n_groups = B * NG
    order = list(range(NT - 1, -1, -1))
    two_filled, two_read, negmax = sc.filled, sc.read, sc.negmax
    QUARTER = S // 4
    USES = STEPS + 2
    AHEAD = STEPS + 1 + NT
    with ExitStack() as ctx:
        def sem(name):
            return ctx.enter_context(nc.semaphore(f"{layer}t_{name}"))

        def sb(name, shape, dt=F32):
            return ctx.enter_context(nc.sbuf_tensor(f"{layer}t_{name}", shape, dt))

        split = sem("split")
        max_loaded = sem("max_loaded")
        t_filled = sem("t_filled")
        exp_done = sem("exp_done")
        masked = sem("masked")
        paired = sem("paired")
        pv_done = sem("pv_done")
        o_copied = sem("o_copied")
        o_step = sem("o_step")
        mom = moment_semaphores(nc, ctx, f"{layer}tm") if masked_after else None
        probs = sb("probs", [P, 4, GH, S])
        turned_max = sb("turned_max", [STEPS, P])
        left = sb("left", [STEPS, P])
        mparts = sb("mparts", [STEPS, PARTS, P], BF16)
        sums = sb("sums", [P, S])
        recip = sb("recip", [P, NT, GH, 1])
        heads = sb("heads", [P, NT, GH, HD])
        pdiag = sb("pdiag", [P, 2, GH, P])
        block = ctx.enter_context(nc.Block())

        PAIRS = [jj for jj in range(1, NT, 2) if masked_after and order[jj]]
        quarters = (2, 3, 0, 1) if masked_after else (0, 1, 2, 3)

        def shared(jj):
            return min(CHUNK, order[jj] * P)

        def added(jj):
            return GH * sum(pair <= jj for pair in PAIRS)

        def pieces_of(jj, quarter):
            j = order[jj]
            lo, hi, edge = quarter * QUARTER, (quarter + 1) * QUARTER, (j + 1) * P
            if not masked_after:
                return [("all", lo, hi)]
            ones = max(lo, shared(jj + 1)) if jj + 1 in PAIRS else lo
            pieces = []
            if min(hi, edge) > ones:
                pieces.append(("ones", ones, min(hi, edge)))
            if hi > max(lo, edge):
                pieces.append(("all", max(lo, edge), hi))
            if lo <= j * P < hi:
                pieces.append(("diagonal", j * P, edge))
            return pieces

        def scores_beside(n_left):
            return STEPS if n_left >= 3 else STEPS - NT if n_left == 2 else 0

        def score_step(v):
            return (1 + (NT + v) // STEPS, (NT + v) // NT % GH, v % NT)

        def uses(n_left, first):
            out = []
            for step in range(STEPS):
                if step < scores_beside(n_left):
                    out.append((step, "score", step))
                if step == NT and not first:
                    out.append((step, "sums", 0))
                if step == STEPS - NT + 1 and n_left >= 2:
                    out.append((step, "max", 0))
            return out

        def uses_before(n, n_left, first):
            if first:
                return AHEAD
            return n * USES + AHEAD - 1 - (NT if n_left == 1 else 0)

        def slot_of(g, first):
            return uses_before(g if g else NG, NG, first) % 2

        uses_in_all = uses_before(n_groups - 1, 1, False) + 1

        def spare(n_left, hh):
            return n_left == 1 and hh % 2 == 1

        def exponent_bank(n_left, hh, half):
            if spare(n_left, hh):
                slot = 1 - slot_of(NG - 1, False)
                return m.ps_two[:, slot, half * CHUNK:(half + 1) * CHUNK]
            return m.ps_one[:, half, :]

        def over_groups(eng, body):
            body(0, 0, n_groups, True)
            with eng.Fori(0, B - 1) as b:
                for g in range(1, NG):
                    body(b, g, NG, False)
                body(b + 1, 0, NG, False)
            for g in range(1, NG):
                body(B - 1, g, NG - g, False)

        @block.sync
        def _(sp):
            def maxima(n, g):
                sp.wait_ge(split, 4 * n + 4)
                for c in range(PARTS):
                    sp.dma_start(m.qx[MAXROW + c:MAXROW + c + 1, g, :, :].rearrange("p h (t q) -> p (h t) q", q=P),
                                 mparts[:, c, :]).then_inc(max_loaded, DMA)

            def body(b, g, n_left, first):
                n = b * NG + g
                if n_left >= 4:
                    if not first:
                        sp.wait_ge(pv_done, STEPS * n)
                    load_group(sp, m, b + (g + 3) // NG, (g + 3) % NG, group_loaded)
                if n_left >= 2:
                    maxima(n + 1, (g + 1) % NG)

            maxima(0, 0)
            over_groups(sp, body)

        @block.gpsimd
        def _(pool):
            def split_max(n, count, first=False):
                hold(pool, two_read, count, m.passed_pool)
                if not first:
                    hold(pool, max_loaded, DMA * PARTS * n, m.passed_pool)
                pool.tensor_copy(mparts[:, 0, :], turned_max[:, :]).then_inc(split, 1)
                pool.wait_ge(split, 4 * n + 1)
                pool.tensor_tensor(left[:, :], turned_max[:, :], mparts[:, 0, :], ALU.subtract).then_inc(split, 1)
                hold(pool, split, 4 * n + 2, m.passed_pool)
                pool.tensor_copy(mparts[:, 1, :], left[:, :]).then_inc(split, 1)
                pool.wait_ge(split, 4 * n + 3)
                pool.tensor_tensor(mparts[:, 2, :], left[:, :], mparts[:, 1, :], ALU.subtract).then_inc(split, 1)

            def body(b, g, n_left, first):
                n = b * NG + g
                for jj, j in enumerate(order):
                    def pair(hh):
                        both = probs[:, jj % 4, hh, 0:shared(jj)]
                        pool.wait_ge(exp_done, (n * STEPS + jj * GH + hh) * 2 + 1)
                        pool.tensor_tensor(both, both, probs[:, jj % 4 - 1, hh, 0:shared(jj)],
                                           ALU.add).then_inc(paired, 1)

                    if jj in PAIRS:
                        for hh in range(GH - 1):
                            pair(hh)
                    if masked_after:
                        pool.wait_ge(exp_done, (n * STEPS + jj * GH + GH) * 2)
                        if not (first and jj < 2):
                            pool.wait_ge(pv_done, n * STEPS + 4 * (jj - 1))
                        pool.tensor_tensor(pdiag[:, jj % 2, :, :], probs[:, jj % 4, :, j * P:(j + 1) * P],
                                           m.causal[:, :].unsqueeze(1).to_broadcast([P, GH, P]),
                                           ALU.mult).then_inc(masked, 1)
                    if jj in PAIRS:
                        pair(GH - 1)
                    if masked_after and g == 0 and not first and jj == 4:
                        for h in range(HALVES):
                            deviations(pool, m, mom, (b - 1) * HALVES + h, h)
                    if jj == 5 and n_left >= 2:
                        done = [kind for _, kind, _ in uses(n_left, first)].index("max") + 1
                        split_max(n + 1, uses_before(n, n_left, first) + done)

            if masked_after:
                pool.sem_inc(mom.rstd_done, 2)
            split_max(0, STEPS + 1, first=True)
            if not masked_after:
                for b in range(B):
                    x = m.x[:, b * NT * D:(b + 1) * NT * D].rearrange("p (t d) -> p t d", d=D)
                    pool.tensor_tensor(x, x, m.b_out[:, :].unsqueeze(1).to_broadcast([P, NT, D]), ALU.add)
            over_groups(pool, body)
            if masked_after:
                for h in range(HALVES):
                    deviations(pool, m, mom, (B - 1) * HALVES + h, h)

        @block.scalar
        def _(act):
            def copy_sums(n, second):
                half = quarters[2 * second] // 2
                act.wait_ge(pv_done, (n + 1) * STEPS - 2 * (1 - second))
                act.activation(sums[:, half * CHUNK:(half + 1) * CHUNK], m.ps_sum[:, half, :],
                               ACT.Copy).then_inc(o_copied, 1)

            def body(b, g, n_left, first):
                n = b * NG + g
                for jj in range(NT):
                    if not (first and jj < 4):
                        act.wait_ge(pv_done, n * STEPS + 4 * (jj - 3))
                        if (jj - 3) % NT in PAIRS:
                            act.wait_ge(paired, n * added(NT) + (added(jj - 3) if jj >= 4 else 0))
                    for hh in range(GH):
                        for half in range(2):
                            act.wait_ge(t_filled, (n * STEPS + jj * GH + hh) * 2 + half + 1)
                            act.activation(probs[:, jj % 4, hh, half * CHUNK:(half + 1) * CHUNK],
                                           exponent_bank(n_left, hh, half), ACT.Exp, scale=SCALE
                                           ).then_inc(exp_done, 1)
                        if not first and (jj, hh) in ((0, 2), (1, 0)):
                            copy_sums(n - 1, jj)

            over_groups(act, body)
            for second in range(2):
                copy_sums(n_groups - 1, second)

        @block.vector
        def _(dve):
            def copy_max(slot, count, n, first=False):
                dve.wait_ge(two_filled, count + 1)
                if not first:
                    dve.wait_ge(split, 4 * n)
                dve.tensor_copy(turned_max[:, :], m.ps_two[0:STEPS, slot, 0:P]).then_inc(two_read, 1)

            def finish(n, b, g, slot, count):
                dve.wait_ge(two_filled, count + 1)
                src = m.ps_two[:, slot, :].rearrange("p (t h r) -> p t h r", t=NT, h=GH)
                dve.reciprocal(recip[:, :, :, :], src[:, :, :, HD:HD + 1]).then_inc(o_step, 1)
                dve.wait_ge(o_step, n * 3 + 1)
                dve.tensor_tensor(heads[:, :, :, :], src[:, :, :, 0:HD],
                                  recip[:, :, :, :].to_broadcast([P, NT, GH, HD]), ALU.mult).then_inc(two_read, 1)
                hold(dve, two_read, count + 1, m.passed_dve)
                dest = m.x if masked_after else m.attn
                cols = dest[:, bass.ds(b * (NT * D), NT * D)]
                cols = cols.rearrange("p (t d) -> p t d", t=NT)[:, :, g * GR:(g + 1) * GR]
                flat = heads[:, :, :, :].rearrange("p t h d -> p t (h d)")
                if masked_after:
                    dve.tensor_tensor(cols, cols, flat, ALU.add).then_inc(o_step, 2)
                else:
                    dve.tensor_copy(cols, flat).then_inc(o_step, 2)

            def sequence_moments(n, b, step):
                h = step // 2
                if step == 0:
                    hold(dve, o_step, n * 3, m.passed_dve)
                (tile_moments if step % 2 else tile_sums)(dve, m, mom, b * HALVES + h, h)

            def body(b, g, n_left, first):
                n = b * NG + g
                finished = None
                for k, (_, kind, v) in enumerate(uses(n_left, first)):
                    count, slot = uses_before(n, n_left, first) + k, (slot_of(g, first) + k) % 2
                    if kind == "score":
                        ahead, hh, i = score_step(v)
                        take_max(dve, m, sc, (g + ahead) % 2, hh, i, slot, count)
                    elif kind == "sums":
                        finish(n - 1, *((b, g - 1) if g else (b - 1, NG - 1)), slot, count)
                        finished = k
                    else:
                        copy_max(slot, count, n + 1)
                    if masked_after and g == 0 and finished is not None and k - finished in (1, 3, 5, 7):
                        sequence_moments(n, b - 1, (k - finished) // 2)

            copy_max(0, STEPS, 0, first=True)
            for i in range(NT):
                take_max(dve, m, sc, 1, 0, i, (i + 1) % 2, STEPS + 1 + i)
            over_groups(dve, body)
            finish(n_groups - 1, B - 1, NG - 1, uses_in_all % 2, uses_in_all)
            if masked_after:
                for step in range(4):
                    sequence_moments(n_groups, B - 1, step)

        @block.tensor
        def _(pe):
            def slot_free(count):
                pe.wait_ge(two_read, count - 1)

            def turn_max(parity, slot, count, later):
                pe.wait_ge(two_read, count - 1 if later else count)
                pe.transpose(m.ps_two[0:STEPS, slot, 0:P], negmax[:, parity, :], m.ident[:, :]
                             ).then_inc(two_filled, 1)

            def turn_sums(n, slot, count):
                pe.wait_ge(o_copied, 2 * n + 2)
                slot_free(count)
                for t in range(NT):
                    last = pe.transpose(m.ps_two[:, slot, t * P:(t + 1) * P], sums[:, t * P:(t + 1) * P],
                                        m.ident[:, :])
                last.then_inc(two_filled, 1)

            def weigh(n, g, jj, turn, first):
                j, quarter = order[jj], quarters[turn]
                half, pieces = quarter // 2, pieces_of(jj, quarter)
                if turn == 0:
                    pe.wait_ge(exp_done, (n * STEPS + jj * GH + GH) * 2)
                if not pieces:
                    return
                clears = quarter % 2 == 0 and not any(pieces_of(before, quarter) for before in range(jj))
                if clears and not first:
                    pe.wait_ge(o_copied, 2 * n - (1 if quarter == quarters[0] else 0))
                if jj in PAIRS and quarter == 0:
                    pe.wait_ge(paired, n * added(NT) + added(jj))
                for k, (kind, q0, q1) in enumerate(pieces):
                    if kind == "diagonal":
                        pe.wait_ge(masked, n * NT + jj + 1)
                    rows = HD if kind == "diagonal" else HD + 1
                    for hh in range(GH):
                        w = m.w01[:, :] if kind == "ones" else m.vg[:, g, j, hh:hh + GH * (rows - 1) + 1:GH]
                        src = pdiag[:, jj % 2, hh, :] if kind == "diagonal" else probs[:, jj % 4, hh, q0:q1]
                        last = pe.matmul(m.ps_sum[32 * hh:32 * hh + rows, half, q0 - half * CHUNK:q1 - half * CHUNK],
                                         w, src, start=clears and k == 0,
                                         stop=jj == NT - 1 and k == len(pieces) - 1, skip_group_check=True)
                empty = 0
                while turn + empty + 1 < 4 and not pieces_of(jj, quarters[turn + empty + 1]):
                    empty += 1
                last.then_inc(pv_done, 1 + empty)

            def body(b, g, n_left, first):
                n = b * NG + g
                todo = uses(n_left, first)
                k = 0

                def exponents(jj, hh, half):
                    u = (n * STEPS + jj * GH + hh) * 2 + half
                    if spare(n_left, hh) and jj == 0 and hh == 1:
                        pe.wait_ge(two_read, uses_before(n, n_left, first))
                    elif n_left == 1 and (jj or hh):
                        pe.wait_ge(exp_done, u - 3)
                    elif not (first and jj == 0 and hh == 0):
                        pe.wait_ge(exp_done, u - 1)
                    pe.matmul(exponent_bank(n_left, hh, half), m.kx[:, g, hh, order[jj] * P:(order[jj] + 1) * P],
                              m.qx[:, g, hh, half * CHUNK:(half + 1) * CHUNK], start=True, stop=True
                              ).then_inc(t_filled, 1)

                pe.wait_ge(max_loaded, DMA * PARTS * (n + 1))
                for step in range(STEPS):
                    jj, hh = divmod(step, GH)
                    exponents(jj, hh, 0)
                    while k < len(todo) and todo[k][0] == step:
                        _, kind, v = todo[k]
                        count, slot = uses_before(n, n_left, first) + k, (slot_of(g, first) + k) % 2
                        if kind == "score":
                            ahead, sh, i = score_step(v)
                            sg = (g + ahead) % NG
                            if sh == 0 and i == 0:
                                pe.wait_ge(group_loaded[sg], DMA * LOADS * (b + (g + ahead) // NG + 1))
                            slot_free(count)
                            score(pe, m, sc, sg, sh, i, slot)
                        elif kind == "sums":
                            turn_sums(n - 1, slot, count)
                        else:
                            turn_max((g + 1) % 2, slot, count, scores_beside(n_left) == STEPS)
                        k += 1
                    exponents(jj, hh, 1)
                    if jj:
                        weigh(n, g, jj - 1, hh, first)
                    elif not first:
                        weigh(n - 1, (g - 1) % NG, NT - 1, hh, False)

            turn_max(0, 0, STEPS, False)
            pe.wait_ge(group_loaded[1], DMA * LOADS)
            for i in range(NT):
                slot_free(STEPS + 1 + i)
                score(pe, m, sc, 1, 0, i, (i + 1) % 2)
            over_groups(pe, body)
            for turn in range(4):
                weigh(n_groups - 1, NG - 1, NT - 1, turn, False)
            turn_sums(n_groups - 1, uses_in_all % 2, uses_in_all)


def project_out(nc, m):
    with ExitStack() as ctx:
        def sem(name):
            return ctx.enter_context(nc.semaphore(f"o_{name}"))

        s = moment_semaphores(nc, ctx, "o")
        copied = sem("copied")
        turned = sem("turned")
        at_done = sem("at_done")
        mixed = sem("mixed")
        added = sem("added")
        block = ctx.enter_context(nc.Block())

        @block.scalar
        def _(act):
            def body(t, low, has):
                if has(2):
                    if low + 2 >= 2:
                        act.wait_ge(turned, t + 1)
                    act.activation(m.xn[:, low % 2, :], m.attn[:, chunk_cols(t + 2)], ACT.Copy).then_inc(copied, 1)
                if has(1):
                    h = (low + 1) % 2
                    act.wait_ge(turned, t + 2)
                    act.activation(m.xt[:, h, :], m.ps_one[:, h, :], ACT.Copy).then_inc(at_done, 1)

            over_chunks(act, body, lead=2)

        @block.tensor
        def _(pe):
            def body(t, low, has):
                if has(1):
                    h = (low + 1) % 2
                    pe.wait_ge(copied, t + 2)
                    for k in range(CT):
                        last = pe.transpose(m.ps_one[:, h, k * P:(k + 1) * P], m.xn[:, h, k * P:(k + 1) * P],
                                            m.ident[:, :])
                    last.then_inc(turned, 1)
                if has(0):
                    h = low % 2
                    pe.wait_ge(at_done, t + 1)
                    if low >= 2:
                        pe.wait_ge(added, t - 1)
                    for k in range(CT):
                        last = pe.matmul(m.ps_two[:, h, k * D:(k + 1) * D], m.xt[:, h, k * P:(k + 1) * P],
                                         m.w_out[:, :], start=True, stop=True, skip_group_check=True)
                    last.then_inc(mixed, 1)

            over_chunks(pe, body, lead=1, start=2)

        @block.gpsimd
        def _(pool):
            pool.sem_inc(s.rstd_done, 2)
            over_chunks(pool, lambda t, low, has: deviations(pool, m, s, t, low % 2))

        @block.vector
        def _(dve):
            def body(t, low, has):
                if has(1):
                    x = m.x[:, chunk_cols(t + 1)]
                    dve.wait_ge(mixed, t + 2)
                    dve.tensor_tensor(x, x, m.ps_two[:, (low + 1) % 2, 0:CHUNK], ALU.add).then_inc(added, 1)
                if has(0):
                    if low >= 0:
                        hold(dve, added, t + 1, m.passed_dve)
                    moments(dve, m, s, t, low % 2)

            over_chunks(dve, body, lead=1)


class ExpertOperands:

    def __init__(self, nc, ctx, layer):
        def sb(name, shape):
            return ctx.enter_context(nc.sbuf_tensor(f"{layer}_{name}", shape, F32R))

        self.x_hi, self.x_lo = (sb(name, [P, B * S]) for name in ("x_hi", "x_lo"))
        self.w_hi, self.w_lo = (sb(name, [P, 2, NE, D]) for name in ("w_hi", "w_lo"))


def route(nc, m, ops, layer):
    with ExitStack() as ctx:
        def sem(name):
            return ctx.enter_context(nc.semaphore(f"{layer}r_{name}"))

        s = norm_semaphores(nc, ctx, f"{layer}r")
        kept = sem("kept")
        x_split = sem("x_split")
        w_high = sem("w_high")
        scored, taken = sem("scored"), sem("taken")
        step, exped, ranked = sem("step"), sem("exped"), sem("ranked")
        room = ctx.enter_context(nc.sbuf_tensor(f"{layer}r_room", [P, (8 * E + 4) * TILES], F32))

        def scratch(n):
            return room[:, n * TILES * E:(n + 1) * TILES * E].rearrange("p (t e) -> p t e", e=E)

        logits, prob, sel, eq, rank, hot, sel2, hot2 = (scratch(n) for n in range(8))
        small = room[:, 8 * TILES * E:].rearrange("p (k t) -> p k t", k=4)
        block = ctx.enter_context(nc.Block())

        @block.gpsimd
        def _(pool):
            for e in range(E):
                pool.memset(rank[:, :, e:e + 1], float(E - e)).then_inc(ranked, 1)
            for n, w in enumerate((m.w1, m.w3)):
                pool.tensor_scalar(ops.w_hi[:, n, :, :], w[:, :, :], 1.0, 0.0, ALU.mult, ALU.add).then_inc(w_high, 1)
                pool.wait_ge(w_high, n + 1)
                pool.tensor_tensor(ops.w_lo[:, n, :, :], w[:, :, :], ops.w_hi[:, n, :, :].bitcast(F32), ALU.subtract)

        @block.scalar
        def _(act):
            def body(t, low, has):
                h = low % 2
                act.wait_ge(s.turned, t + 1)
                if low >= 2:
                    act.wait_ge(scored, t - 1)
                act.activation(m.xt[:, h, :], m.ps_one[:, h, :], ACT.Copy).then_inc(s.xt_done, 1)
                act.activation(ops.x_hi[:, chunk_cols(t)], m.ps_one[:, h, :], ACT.Copy).then_inc(kept, 1)

            over_chunks(act, body, start=2)
            act.wait_ge(step, 2)
            act.activation(prob, prob, ACT.Exp).then_inc(exped, 1)

        @block.tensor
        def _(pe):
            def body(t, low, has):
                if has(1):
                    if low + 1 >= 2:
                        pe.wait_ge(x_split, t)
                    norm_pe_turn(pe, m, s, t + 1, low + 1)
                if has(0):
                    h = low % 2
                    pe.wait_ge(s.xt_done, t + 1)
                    if low >= 2:
                        pe.wait_ge(taken, t - 1)
                    for k in range(CT):
                        last = pe.matmul(m.ps_sum[:, h, k * E:(k + 1) * E], m.xt[:, h, k * P:(k + 1) * P],
                                         m.w_router[:, :], start=True, stop=True, skip_group_check=True)
                    last.then_inc(scored, 1)

            over_chunks(pe, body, lead=1, start=2)

        @block.vector
        def _(dve):
            flat = room[:, 0:TILES * E]
            def body(t, low, has):
                if has(0):
                    dve.wait_ge(kept, t + 1)
                    dve.tensor_tensor(ops.x_lo[:, chunk_cols(t)], m.ps_one[:, low % 2, :],
                                      ops.x_hi[:, chunk_cols(t)].bitcast(F32), ALU.subtract).then_inc(x_split, 1)
                if has(2):
                    norm_dve_apply(dve, m, s, t + 2, low + 2)
                if has(0):
                    dve.wait_ge(scored, t + 1)
                    dve.tensor_copy(flat[:, bass.ds(t * (CT * E), CT * E)], m.ps_sum[:, low % 2, 0:CT * E]
                                    ).then_inc(taken, 1)

            over_chunks(dve, body, lead=2)

            def wide(k):
                return small[:, k, :].unsqueeze(2).to_broadcast([P, TILES, E])

            done = [0]

            def chain(ins):
                done[0] += 1
                ins.then_inc(step, 1)
                dve.wait_ge(step, done[0])

            dve.wait_ge(taken, CHUNKS)
            chain(dve.tensor_reduce(small[:, 0, :], logits, AX.X, ALU.max))
            chain(dve.tensor_tensor(prob, logits, wide(0), ALU.subtract))
            dve.wait_ge(exped, 1)
            chain(dve.tensor_reduce(small[:, 1, :], prob, AX.X, ALU.add))
            chain(dve.reciprocal(small[:, 1, :], small[:, 1, :]))
            chain(dve.tensor_tensor(prob, prob, wide(1), ALU.mult))
            bias = m.e_bias[:, :].unsqueeze(1).to_broadcast([P, TILES, E])
            chain(dve.tensor_tensor(sel, prob, bias, ALU.add))
            dve.wait_ge(ranked, E)
            for src, out in ((sel, hot), (sel2, hot2)):
                chain(dve.tensor_reduce(small[:, 2, :], src, AX.X, ALU.max))
                chain(dve.tensor_tensor(eq, src, wide(2), ALU.is_equal))
                chain(dve.tensor_tensor(eq, eq, rank, ALU.mult))
                chain(dve.tensor_reduce(small[:, 3, :], eq, AX.X, ALU.max))
                chain(dve.tensor_tensor(out, rank, wide(3), ALU.is_equal))
                if out is hot:
                    chain(dve.scalar_tensor_tensor(sel2, hot, -3.0e38, sel, ALU.mult, ALU.add))
            chain(dve.tensor_tensor(hot, hot, hot2, ALU.add))
            chain(dve.tensor_tensor(m.gates[:, :, 0:E], hot, prob, ALU.mult))


def experts(nc, m, ops, layer, out, loads):
    last_layer = out is not None
    UNITS = HALVES * NE
    with ExitStack() as ctx:
        def sem(name):
            return ctx.enter_context(nc.semaphore(f"{layer}e_{name}"))

        def sb(name, shape, dt=F32):
            return ctx.enter_context(nc.sbuf_tensor(f"{layer}e_{name}", shape, dt))

        h_done = sem("h_done")
        s_done = sem("s_done")
        a_done = sem("a_done")
        y_done = sem("y_done")
        acc_done = sem("acc_done")
        begun = sem("begun")
        if last_layer:
            stored = [sem(f"stored{h}") for h in range(2)]
            acc_free = sem("acc_free")
        else:
            loaded = sem("loaded")
            put = sem("put")
            s = moment_semaphores(nc, ctx, f"{layer}e")
        silu, hid = m.xn, m.xt
        acc = sb("acc", [P, 2, CHUNK])
        gate = sb("gate", [P, 2, CT, NE])
        gates_flat = m.gates[:, :, :].rearrange("p t e -> p (t e)")
        block = ctx.enter_context(nc.Block())

        @block.tensor
        def _(pe):
            def hidden(b, k):
                h, e = divmod(k, NE)
                x_hi, x_lo = (x[:, bass.ds((b * 2 + h) * CHUNK, CHUNK)] for x in (ops.x_hi, ops.x_lo))
                for w in range(2):
                    for i, (weights, x) in enumerate(((ops.w_hi, x_hi), (ops.w_hi, x_lo), (ops.w_lo, x_hi))):
                        last = pe.matmul(m.ps_two[:, k % 2, w * CHUNK:(w + 1) * CHUNK], weights[:, w, e, :], x, start=i == 0, stop=i == 2)
                last.then_inc(h_done, 1)

            def output(b, k):
                e, unit = k % NE, b * UNITS + k
                pe.wait_ge(a_done, unit + 1)
                pe.wait_ge(acc_done, (unit + 1) * CT)
                for t in range(CT):
                    last = pe.matmul(m.ps_one[:, k % 2, t * D:(t + 1) * D], hid[:, k % 2, t * P:(t + 1) * P],
                                     m.w2[:, e, :], start=True, stop=True, skip_group_check=True)
                last.then_inc(y_done, 1)

            def body(b, last=False):
                for k in range(UNITS):
                    if k + 1 < UNITS:
                        hidden(b, k + 1)
                    elif not last:
                        hidden(b + 1, 0)
                    output(b, k)

            hidden(0, 0)
            with pe.Fori(0, B - 1) as b:
                body(b)
            body(B - 1, last=True)

        @block.scalar
        def _(act):
            with act.Fori(0, B) as b:
                for k in range(UNITS):
                    act.wait_ge(h_done, b * UNITS + k + 1)
                    act.activation(silu[:, k % 2, :], m.ps_two[:, k % 2, 0:CHUNK], ACT.Silu).then_inc(s_done, 1)

        if not last_layer:
            @block.gpsimd
            def _(pool):
                pool.sem_inc(s.rstd_done, 2)
                over_chunks(pool, lambda t, low, has: deviations(pool, m, s, t, low % 2))

        @block.vector
        def _(dve):
            def begin(b, h):
                chunk = b * 2 + h
                if last_layer:
                    dve.wait_ge(acc_free, chunk + 1)
                dve.tensor_copy(acc[:, h, :], m.x[:, chunk_cols(chunk)]).then_inc(begun, 1)
                dve.tensor_copy(gate[:, h, :, :].rearrange("p t e -> p (t e)"),
                                gates_flat[:, bass.ds(chunk * (CT * NE), CT * NE)]).then_inc(begun, 1)

            def gather(b, k):
                h, e = divmod(k, NE)
                before = (b * UNITS + k) * CT
                dve.wait_ge(y_done, b * UNITS + k + 1)
                if e == 0:
                    dve.wait_ge(begun, (b * 2 + h) * 2 + 2)
                dve.wait_ge(acc_done, before + 2 * CT)
                for t in range(CT):
                    part = acc[:, h, t * D:(t + 1) * D]
                    dve.scalar_tensor_tensor(part, m.ps_one[:, k % 2, t * D:(t + 1) * D], gate[:, h, t, e:e + 1],
                                             part, ALU.mult, ALU.add).then_inc(acc_done, 1)

            def finish(b, h, step):
                chunk = b * 2 + h
                if step == 0:
                    hold(dve, acc_done, (b * UNITS + (h + 1) * NE + 2) * CT, m.passed_dve)
                    dve.tensor_copy(m.x[:, chunk_cols(chunk)], acc[:, h, :]).then_inc(put, 1)
                elif step == 1:
                    dve.wait_ge(put, chunk + 1)
                    tile_sums(dve, m, s, chunk, h)
                else:
                    tile_moments(dve, m, s, chunk, h)

            def body(b, first=False, last=False):
                for k in range(UNITS):
                    dve.wait_ge(s_done, b * UNITS + k + 1)
                    dve.tensor_tensor(hid[:, k % 2, :], silu[:, k % 2, :], m.ps_two[:, k % 2, CHUNK:2 * CHUNK],
                                      ALU.mult).then_inc(a_done, 1)
                    if k:
                        gather(b, k - 1)
                    elif not first:
                        gather(b - 1, UNITS - 1)
                    if not last_layer and k < 3 and not first:
                        finish(b - 1, 1, k)
                    if not last_layer and NE <= k < NE + 3:
                        finish(b, 0, k - NE)
                    if k == NE // 2:
                        begin(b, 1)
                    if k == NE + NE // 2 and not last:
                        begin(b + 1, 0)

            dve.sem_inc(acc_done, 2 * CT)
            begin(0, 0)
            body(0, first=True)
            with dve.Fori(0, B - 2) as b:
                body(b + 1)
            body(B - 1, last=True)
            gather(B - 1, UNITS - 1)
            if not last_layer:
                for step in range(3):
                    finish(B - 1, 1, step)

        @block.sync
        def _(sp):
            if last_layer:
                sp.sem_inc(acc_free, 2)
                rows = out.rearrange("b (h t p) d -> p b h t d", p=P, t=CT)
                with sp.Fori(0, B) as b:
                    for h in range(2):
                        sp.wait_ge(acc_done, (b * UNITS + (h + 1) * NE + 2) * CT)
                        sp.dma_start(rows[:, bass.ds(b, 1), h, :, :].rearrange("p b t d -> p (b t) d"),
                                     acc[:, h, :].rearrange("p (t d) -> p t d", t=CT)).then_inc(stored[h], DMA)
                        sp.wait_ge(stored[h], DMA * (b + 1))
                        sp.sem_inc(acc_free, 1)
            else:
                for dst, src in loads:
                    sp.dma_start(dst, src).then_inc(loaded, DMA)
                sp.wait_ge(loaded, DMA * len(loads))


def build(nc, a, out):
    with ExitStack() as ctx:
        m = allocate(nc, ctx)
        group_loaded = {layer: [ctx.enter_context(nc.semaphore(f"{layer}_group_loaded{g}")) for g in range(NG)]
                        for layer in "ab"}
        scores = {layer: Scores(nc, ctx, layer) for layer in "ab"}
        expert_loads = [
            (m.w_out[:, :], a["b_wout"]), (m.b_out[:, :], a["b_bias"].partition_broadcast(P)),
            (m.w_router[:, :], a["router"]), (m.e_bias[:, :], a["e_bias"].partition_broadcast(P)),
        ]
        for w, routed, shared in ((m.w1, "w1", "sw1"), (m.w3, "w3", "sw3"), (m.w2, "w2", "sw2")):
            expert_loads += [(w[:, 0:E, :], a[routed].rearrange("e i o -> i e o")), (w[:, E, :], a[shared])]
        setup(nc, m, a)
        project(nc, m, "a", expert_loads, group_loaded["a"], scores["a"])
        attend(nc, m, "a", group_loaded["a"], scores["a"])
        with ExitStack() as ffn:
            ops = ExpertOperands(nc, ffn, "a")
            route(nc, m, ops, "a")
            experts(nc, m, ops, "a", None, [
                (m.w_q[:, 0, 0, :], a["b_wq"]), (m.w_q[:, 1, 0, :], a["b_wk"]),
                (m.w_q[:, 0, 1, :], a["b_wq_swapped"]), (m.w_q[:, 1, 1, :], a["b_wk_swapped"]),
                (m.w_v[:, :], a["b_wv"]), (m.rope, a["rope"]),
            ])
        project(nc, m, "b", [], group_loaded["b"], scores["b"])
        attend(nc, m, "b", group_loaded["b"], scores["b"])
        project_out(nc, m)
        with ExitStack() as ffn:
            ops = ExpertOperands(nc, ffn, "b")
            route(nc, m, ops, "b")
            experts(nc, m, ops, "b", out, [])




def _layout(i):
    perm = np.arange(D).reshape(NG, GH, HD).transpose(0, 2, 1).reshape(-1)
    swap = np.roll(np.arange(D).reshape(NG, GH, HD), HD // 2, axis=2).transpose(0, 2, 1).reshape(-1)
    qkv = np.asarray(i["L0_attn_b_w_qkv"]).T
    wq, wk, wv = qkv[:, 0:D], qkv[:, D:2 * D], qkv[:, 2 * D:3 * D]
    return {
        "x": i["L0_attn_a_content"],
        "a_wq": i["L0_attn_a_Wq"][:, perm], "a_wk": i["L0_attn_a_Wk"][:, perm], "a_wv": i["L0_attn_a_Wv"][:, perm],
        "b_wq": wq[:, perm], "b_wk": wk[:, perm], "b_wv": wv[:, perm],
        "b_wq_swapped": wq[:, swap], "b_wk_swapped": wk[:, swap],
        "b_wout": np.asarray(i["L0_attn_b_w_out"]).T, "b_bias": i["L0_attn_b_b_out"],
        "router": i["L0_ffn_router_w"], "e_bias": i["L0_ffn_expert_bias"],
        "w1": i["L0_ffn_w1"], "w2": i["L0_ffn_w2"], "w3": i["L0_ffn_w3"],
        "sw1": i["L0_ffn_sw1"], "sw2": i["L0_ffn_sw2"], "sw3": i["L0_ffn_sw3"],
    }


def _rope_tables():
    half = HD // 2
    inv = (1.0 / 10000.0 ** (np.arange(0, HD, 2, dtype=np.float32) / np.float32(HD))).astype(np.float32)
    angle = (np.arange(S, dtype=np.float32)[:, None] * inv[None, :]).astype(np.float32).astype(np.float64)
    cos, sin = np.cos(angle).T, np.sin(angle).T
    rows = np.stack([np.concatenate([cos, cos]), np.concatenate([-sin, sin])])
    rows = np.broadcast_to(rows[:, None, :, None, :], (2, NG, 2 * half, GH, S)).reshape(2, P, S)
    return np.ascontiguousarray(rows.transpose(1, 0, 2)).astype(np.float32)


def kernel(**inputs):
    import concourse.bacc as bacc
    from concourse.bass_utils import run_bass_kernel_spmd

    nc = bacc.Bacc("TRN2", target_bir_lowering=False, num_devices=1)
    arrays = {f"in_{k}": np.ascontiguousarray(v) for k, v in _layout({k: np.asarray(v) for k, v in inputs.items()}).items()}
    arrays["in_rope"] = _rope_tables()
    args = {k[3:]: nc.dram_tensor(k, v.shape, F32, kind="ExternalInput").ap() for k, v in arrays.items()}
    out = nc.dram_tensor("out_dram", (B, S, D), F32, kind="ExternalOutput").ap()
    build(nc, args, out)
    r = run_bass_kernel_spmd(nc, [arrays], core_ids=[0])
    return r.results[0]["out_dram"]
```
